# Optimizing a Trainium2 kernel written in Bass

```python
import numpy as np
import jax
import jax.numpy as jnp

def _softmax(x, axis=-1):
    return jax.nn.softmax(x, axis=axis)

def _gelu(x):
    return jax.nn.gelu(x, approximate=True)

def _silu(x):
    return jax.nn.silu(x)

def _sigmoid(x):
    return jax.nn.sigmoid(x)

def _layernorm(x, axis=-1, eps=1e-05):
    m = jnp.mean(x, axis=axis, keepdims=True)
    v = jnp.var(x, axis=axis, keepdims=True)
    return (x - m) / jnp.sqrt(v + eps)

def _scatter_add(tgt, idx, src, axis=0):
    return tgt.at[idx].add(src)

def _segment_sum(src, seg, n):
    return jax.ops.segment_sum(src, seg, n)
kernel_name = 'mk_gnn_preln_d4_gnn_r8_c72687'

def setup_inputs(seed: int=0):
    np.random.seed(seed)
    _w = jnp.asarray

    def _rec_inputs():
        import jax
        import jax.numpy as jnp
        _gk = jax.random.key(seed)
        x = -0.0003713 + 1 * jax.random.normal(jax.random.fold_in(_gk, 1), (12500, 128), jnp.float32)
        _s = jax.random.randint(jax.random.fold_in(_gk, 2), (100000,), 0, 12500, jnp.int32)
        _d = jax.random.randint(jax.random.fold_in(_gk, 3), (100000,), 0, 12500, jnp.int32)
        _loop = jnp.arange(12500, dtype=jnp.int32)
        src = jnp.concatenate([_s, _d, _loop])
        dst = jnp.concatenate([_d, _s, _loop])
        _o = jnp.argsort(dst, stable=True)
        src = src[_o]
        dst = dst[_o]
        edge_type_8 = jax.random.randint(jax.random.fold_in(_gk, 13), (212500,), 0, 8, jnp.int32)
        return (x, src, dst, edge_type_8)
    x, src, dst, edge_type_8 = _rec_inputs()

    def _L0_gnn_setup():
        import jax, jax.numpy as jnp
        import numpy as np
        N_NODES = 12500
        N_EDGES = 200000
        N_RELS = 8
        IN_DIM = HID_DIM = OUT_DIM = 128

        def _rel_graph_conv(x, W, W_loop, b, src, dst, etypes, num_nodes):
            xw = jnp.einsum('nd,rdh->rnh', x, W)
            msg = xw[etypes, src]
            agg = jax.ops.segment_sum(msg, dst, num_segments=num_nodes)
            return agg + x @ W_loop + b
        key = jax.random.key(seed)
        ks = jax.random.split(key, 8)
        s = 1.0 / np.sqrt(IN_DIM)
        return {'features': jax.random.normal(ks[0], (N_NODES, IN_DIM), jnp.float32), 'W1': jax.random.normal(ks[1], (N_RELS, IN_DIM, HID_DIM), jnp.float32) * s, 'loop1': jax.random.normal(ks[2], (IN_DIM, HID_DIM), jnp.float32) * s, 'b1': jnp.zeros((HID_DIM,), jnp.float32), 'W2': jax.random.normal(ks[3], (N_RELS, HID_DIM, OUT_DIM), jnp.float32) * s, 'loop2': jax.random.normal(ks[4], (HID_DIM, OUT_DIM), jnp.float32) * s, 'b2': jnp.zeros((OUT_DIM,), jnp.float32), 'src': jax.random.randint(ks[5], (N_EDGES,), 0, N_NODES, jnp.int32), 'dst': jax.random.randint(ks[6], (N_EDGES,), 0, N_NODES, jnp.int32), 'etypes': jax.random.randint(ks[7], (N_EDGES,), 0, N_RELS, jnp.int32)}
    _L0_gnn_all = _L0_gnn_setup()
    _L0_gnn_in = {k: v for k, v in _L0_gnn_all.items() if k in ('W1', 'loop1', 'b1', 'W2', 'loop2', 'b2')}
    del _L0_gnn_all

    def _L1_gnn_setup():
        import jax, jax.numpy as jnp
        import numpy as np
        N = 12500
        E = 200000
        D_IN = 128
        D_OUT = 128
        BN_EPS = 1e-05
        key = jax.random.key(seed)
        k1, k2, k3, k4 = jax.random.split(key, 4)
        x = jax.random.normal(k1, (N, D_IN), dtype=jnp.float32)
        edge_index = jax.random.randint(k2, (2, E), 0, N, dtype=jnp.int64)
        lim = 1.0 / np.sqrt(D_IN)
        W = jax.random.uniform(k3, (D_OUT, D_IN), minval=-lim, maxval=lim, dtype=jnp.float32)
        b = jax.random.uniform(k4, (D_OUT,), minval=-lim, maxval=lim, dtype=jnp.float32)
        gamma = jnp.ones((D_OUT,), dtype=jnp.float32)
        beta = jnp.zeros((D_OUT,), dtype=jnp.float32)
        return {'x': x, 'edge_index': edge_index, 'W': W, 'b': b, 'gamma': gamma, 'beta': beta, 'batch_size': 32}
    _L1_gnn_all = _L1_gnn_setup()
    _L1_gnn_in = {k: v for k, v in _L1_gnn_all.items() if k in ('W', 'b', 'gamma', 'beta')}
    del _L1_gnn_all

    def _L2_gnn_setup():
        import jax, jax.numpy as jnp
        import numpy as np
        N_NODES = 12500
        N_EDGES = 200000
        F_IN = 128
        N_HEADS = 4
        F_HID = 32
        NEG_SLOPE = 0.2
        key = jax.random.key(seed)
        k1, k2, k3, k4, k5 = jax.random.split(key, 5)
        node_features = jax.random.normal(k1, (N_NODES, F_IN), dtype=jnp.float32)
        edge_index = jax.random.randint(k2, (2, N_EDGES), 0, N_NODES, dtype=jnp.int64)
        W = jax.random.normal(k3, (F_IN, N_HEADS * F_HID), dtype=jnp.float32) * 0.05
        b = jax.random.normal(k4, (N_HEADS * F_HID,), dtype=jnp.float32) * 0.05
        attn = jax.random.normal(k5, (1, N_HEADS, 2 * F_HID), dtype=jnp.float32) * 0.1
        return {'node_features': node_features, 'edge_index': edge_index, 'W': W, 'b': b, 'attn': attn}
    _L2_gnn_all = _L2_gnn_setup()
    _L2_gnn_in = {k: v for k, v in _L2_gnn_all.items() if k in ('W', 'b', 'attn')}
    del _L2_gnn_all

    def _L3_gnn_setup():
        import jax, jax.numpy as jnp
        import numpy as np
        N_NODES = 12500
        key = jax.random.key(seed)
        k1, k2, k3 = jax.random.split(key, 3)
        x = jax.random.normal(k1, (N_NODES, 128), dtype=jnp.float32)
        edge_src = jax.random.randint(k2, (80000,), 0, N_NODES, dtype=jnp.int64)
        edge_dst = jax.random.randint(k3, (80000,), 0, N_NODES, dtype=jnp.int64)
        return {'x': x, 'edge_src': edge_src, 'edge_dst': edge_dst}
    _L3_gnn_all = _L3_gnn_setup()
    _L3_gnn_in = {k: v for k, v in _L3_gnn_all.items() if k in ()}
    del _L3_gnn_all
    return {'x': x, 'src': src, 'dst': dst, 'edge_type_8': edge_type_8, 'L0_gnn_W1': _L0_gnn_in['W1'], 'L0_gnn_loop1': _L0_gnn_in['loop1'], 'L0_gnn_b1': _L0_gnn_in['b1'], 'L0_gnn_W2': _L0_gnn_in['W2'], 'L0_gnn_loop2': _L0_gnn_in['loop2'], 'L0_gnn_b2': _L0_gnn_in['b2'], 'L1_gnn_W': _L1_gnn_in['W'], 'L1_gnn_b': _L1_gnn_in['b'], 'L1_gnn_gamma': _L1_gnn_in['gamma'], 'L1_gnn_beta': _L1_gnn_in['beta'], 'L2_gnn_W': _L2_gnn_in['W'], 'L2_gnn_b': _L2_gnn_in['b'], 'L2_gnn_attn': _L2_gnn_in['attn']}

def reference(x, src, dst, edge_type_8, L0_gnn_W1, L0_gnn_loop1, L0_gnn_b1, L0_gnn_W2, L0_gnn_loop2, L0_gnn_b2, L1_gnn_W, L1_gnn_b, L1_gnn_gamma, L1_gnn_beta, L2_gnn_W, L2_gnn_b, L2_gnn_attn):
    import jax
    import jax.numpy as jnp

    def _L0_gnn_ref(features, W1, loop1, b1, W2, loop2, b2, src, dst, etypes):
        import jax, jax.numpy as jnp
        import numpy as np
        N_NODES = 12500
        N_EDGES = 200000
        N_RELS = 8
        IN_DIM = HID_DIM = OUT_DIM = 128

        def _rel_graph_conv(x, W, W_loop, b, src, dst, etypes, num_nodes):
            xw = jnp.einsum('nd,rdh->rnh', x, W)
            msg = xw[etypes, src]
            agg = jax.ops.segment_sum(msg, dst, num_segments=num_nodes)
            return agg + x @ W_loop + b
        n = features.shape[0]
        h = _rel_graph_conv(features, W1, loop1, b1, src, dst, etypes, n)
        h = jax.nn.relu(h)
        h = _rel_graph_conv(h, W2, loop2, b2, src, dst, etypes, n)
        return h

    def _L1_gnn_ref(x, edge_index, W, b, gamma, beta, batch_size):
        import jax, jax.numpy as jnp
        import numpy as np
        N = 12500
        E = 200000
        D_IN = 128
        D_OUT = 128
        BN_EPS = 1e-05
        h = x @ W.T + b
        num_nodes = h.shape[0]
        row, col = (edge_index[0], edge_index[1])
        agg = jax.ops.segment_sum(h[col], row, num_segments=num_nodes)
        cnt = jax.ops.segment_sum(jnp.ones((edge_index.shape[1], 1), dtype=h.dtype), row, num_segments=num_nodes)
        agg = agg / (cnt + 1e-08)
        h = h + agg
        mean = jnp.mean(h, axis=0)
        var = jnp.mean((h - mean) ** 2, axis=0)
        out = (h - mean) * jax.lax.rsqrt(var + BN_EPS) * gamma + beta
        return out

    def _L2_gnn_ref(node_features, edge_index, W, b, attn):
        import jax, jax.numpy as jnp
        import numpy as np
        N_NODES = 12500
        N_EDGES = 200000
        F_IN = 128
        N_HEADS = 4
        F_HID = 32
        NEG_SLOPE = 0.2
        N = node_features.shape[0]
        h = (node_features @ W + b).reshape(N, N_HEADS, F_HID)
        tgt = edge_index[0]
        src = edge_index[1]
        a_i = attn[0, :, :F_HID]
        a_j = attn[0, :, F_HID:]
        s_i = jnp.einsum('nhf,hf->nh', h, a_i)
        s_j = jnp.einsum('nhf,hf->nh', h, a_j)
        eij = jax.nn.leaky_relu(s_i[tgt] + s_j[src], negative_slope=NEG_SLOPE)
        m = jax.ops.segment_max(eij, tgt, num_segments=N)
        ex = jnp.exp(eij - m[tgt])
        denom = jax.ops.segment_sum(ex, tgt, num_segments=N)
        alpha = ex / denom[tgt]
        msg = alpha[:, :, None] * h[src]
        out = jax.ops.segment_sum(msg, tgt, num_segments=N)
        out = out + h
        return out.reshape(N, N_HEADS * F_HID)

    def _L3_gnn_ref(x, edge_src, edge_dst):
        import jax, jax.numpy as jnp
        import numpy as np
        N_NODES = 12500
        n = x.shape[0]
        gathered = x[edge_src]
        sums = jax.ops.segment_sum(gathered, edge_dst, num_segments=n)
        counts = jax.ops.segment_sum(jnp.ones(edge_dst.shape, dtype=x.dtype), edge_dst, num_segments=n)
        denom = jnp.maximum(counts, 1.0)[:, None]
        return sums / denom
    edge_index = jnp.stack([src, dst])
    h = jnp.maximum(_layernorm(x, axis=-1), 0.0)
    x = x + _L0_gnn_ref(h, L0_gnn_W1, L0_gnn_loop1, L0_gnn_b1, L0_gnn_W2, L0_gnn_loop2, L0_gnn_b2, src, dst, edge_type_8)
    h = jnp.maximum(_layernorm(x, axis=-1), 0.0)
    x = x + _L1_gnn_ref(h, edge_index, L1_gnn_W, L1_gnn_b, L1_gnn_gamma, L1_gnn_beta, 32)
    h = jnp.maximum(_layernorm(x, axis=-1), 0.0)
    x = x + _L2_gnn_ref(h, edge_index, L2_gnn_W, L2_gnn_b, L2_gnn_attn)
    h = jnp.maximum(_layernorm(x, axis=-1), 0.0)
    x = x + _L3_gnn_ref(h, src, dst)
    return x

_drawn_inputs = setup_inputs


def setup_inputs(seed=0):
    import zlib

    import numpy as np

    out = dict(_drawn_inputs(seed))
    spreads = {'L0_gnn_b1': (0.0, 0.1),
     'L0_gnn_b2': (0.0, 0.8),
     'L1_gnn_gamma': (1.0, 0.6),
     'L1_gnn_beta': (0.0, 0.8)}
    factors = {'L1_gnn_b': 8.0, 'L2_gnn_b': 8.0, 'L2_gnn_attn': 8.0}
    for name, (base, spread) in spreads.items():
        noise = np.random.default_rng([zlib.crc32(name.encode()), seed]).standard_normal(out[name].shape)
        drawn = base * np.exp(spread * noise) if base else spread * noise
        out[name] = jnp.asarray(drawn.astype(out[name].dtype))
    for name, factor in factors.items():
        out[name] = (out[name] * factor).astype(out[name].dtype)
    return out
```

```python
import concourse.bass as bass
from concourse import mybir
from contextlib import ExitStack

F32, I32, BF16 = mybir.dt.float32, mybir.dt.int32, mybir.dt.bfloat16
ALU = mybir.AluOpType
ACT = mybir.ActivationFunctionType
AX = mybir.AxisListType

P = 128
N, D, E, R = 12500, 128, 212500, 8
HEADS, HD = 4, 32
NB = -(-N // P)
LAST = N - (NB - 1) * P
ET = -(-E // P)
TAIL = E - (ET - 1) * P
EP = 125
EC = E // EP
K = 8
RING = 4
MAX_STEPS = ET + NB - 1
NG = -(-MAX_STEPS // (K * RING)) * RING
NS = NG * K
SC = -(-NS // P)
SW = SC * P
RW = D + HEADS
ROWS = NB * P
EROWS = ET * P
LN_EPS = BN_EPS = 1e-5
SLOPE = 0.2
BIG = 1e30
FAR = float(1 << 20)
CH = 14
NCH = NB // CH


class Chain:

    def __init__(self, eng, sem):
        self.eng, self.sem, self.n, self.at = eng, sem, 0, 0

    def inc(self, ins):
        ins.then_inc(self.sem, 1)
        self.n += 1
        return ins

    def hold(self):
        self.eng.wait_ge(self.sem, self.at + self.n)

    def step(self, ins):
        self.inc(ins)
        self.hold()

    def enter(self, i, per):
        self.outer, self.per = self.n, per
        self.at, self.n = self.outer + i * per, 0

    def leave(self, times):
        assert self.n == self.per, (self.n, self.per)
        self.n, self.at = self.outer + times * self.per, 0


def build_gnn(nc, x, src, dst, etype, W1, loop1, b1, W2, loop2, b2, lw, lb, gamma, beta, gw, gb, attn, out):
    ctx = ExitStack()
    sb = lambda name, shape, dt=F32: ctx.enter_context(nc.sbuf_tensor(name, shape, dt))
    pb = lambda name: ctx.enter_context(nc.psum_tensor(name, [P, 512], F32))
    sem = lambda name: ctx.enter_context(nc.semaphore(name))
    dram = lambda name, shape, dt=F32: nc.dram_tensor(name, shape, dt, kind="Internal").ap()

    with ctx:
        X = sb("X", [P, NB, D])
        ACC = sb("ACC", [P, NB, RW])
        IDXA = sb("IDXA", [P, SW], I32)
        DLOA = sb("DLOA", [P, SW])
        DSTA = sb("DSTA", [P, SW])
        POSA = sb("POSA", [P, SW])
        IDXB = DSTA[:].bitcast(I32)
        SLOB = sb("SLOB", [P, SW])
        BREGA = sb("BREGA", [1, SW], I32)
        BREGB = sb("BREGB", [1, SW], I32)
        TREGB = sb("TREGB", [1, SW], I32)
        G = sb("G", [P, RING, K, RW])
        OH = sb("OH", [P, 2, K, P])
        IDS = sb("IDS", [P, RING, K], I32)
        WT = sb("WT", [P, (R + 1) * D])
        BIAS = sb("BIAS", [P, RW + HEADS])
        IOTA = sb("IOTA", [P, P])
        PCOL = sb("PCOL", [P, 1])
        IDENT = sb("IDENT", [P, P])
        UST = sb("UST", [P, P])
        USTB = sb("USTB", [P, P], BF16)
        LINB = sb("LINB", [P, P], BF16)
        ONES = sb("ONES", [P, P])
        CNTB = sb("CNTB", [EP, NB + 1])
        ST6 = sb("ST6", [P, NB, 6])
        MV = sb("MV", [P, NB, 2])
        RSTD, NMR = sb("RSTD", [P, NB]), sb("NMR", [P, NB])
        SCR = sb("SCR", [P, 4, 4 * P])
        HB, HT = sb("HB", [P, 2, D]), sb("HT", [P, 2, D])
        SM = sb("SM", [P, 6, K * HEADS])
        SI = sb("SI", [P, NB, 2 * HEADS])
        MJ = sb("MJ", [P, NB, HEADS])
        PS = [pb(f"PS{i}") for i in range(8)]
        TAB = dram("TAB", [ROWS * R, D])
        HROW = dram("HROW", [ROWS, RW])
        ET1 = dram("ET1", [ET, 3 * P], I32)
        MSG = dram("MSG", [EROWS, RW])
        KEEP = dram("KEEP", [NG, P, K * RW])

        def bcast(ap, *shape):
            return ap.broadcast_to(list(shape))

        words = ACC[:].rearrange("p b w -> p (b w)")
        used = [0]

        def part(n):
            a = words[:, used[0]:used[0] + n]
            used[0] += n
            return a

        s_ld = [sem(f"s_ld{i}") for i in range(5)]
        s_k, s_pk, s_v = sem("s_k"), sem("s_pk"), sem("s_v")
        s_pe, s_eg, s_tix = sem("s_pe"), sem("s_eg"), sem("s_tix")
        EDG = [part(EC), part(EC)]
        EDF = part(EC)
        SELX, ITER, TMPW = part(SW), part(SW), part(SW)
        EGI = [part(3 * P).bitcast(I32) for _ in range(2)]
        EGF = part(3 * P)
        JUNK = OH[:].rearrange("p a k n -> p (a k n)")[:, 0:EC]
        IOTI = G[:].rearrange("p r k w -> p (r k w)")[:, 0:SW].bitcast(I32)
        small = SCR[:].rearrange("p a c -> p (a c)")
        taken = [0]

        def cut(rows, n):
            a = small[0:rows, taken[0]:taken[0] + n]
            taken[0] += n
            return a

        THR, CNTA, ISTEP = cut(P, NB + 1), cut(EP, NB + 1), cut(P, SC)
        SE, FL, COL, RH = cut(NB, 2), cut(NB, 2).bitcast(I32), cut(NB, 8), cut(NB, 2)
        BW = cut(NB, 2 * P).rearrange("p (a c) -> p a c", a=2)
        TIX = cut(P, SC).bitcast(I32)
        TAILI = cut(1, 3 * P).bitcast(I32)
        MTAIL = cut(P - TAIL, RW)
        n_full = (ET - 1) * P
        with nc.Block() as block:
            @block.sync
            def _(q):
                q.dma_start(EDG[0][0:EP, :].bitcast(I32), dst.rearrange("(p c) -> p c", p=EP)).then_inc(s_ld[0], 16)
                q.dma_start(EDG[1][0:EP, :].bitcast(I32), src.rearrange("(p c) -> p c", p=EP)).then_inc(s_ld[1], 16)
                q.dma_start(X[:, 0:NB - 1, :], x[0:(NB - 1) * P, :].rearrange("(b p) d -> p b d", p=P)).then_inc(s_ld[2], 16)
                q.wait_ge(s_v, 1)
                q.dma_start(X[0:LAST, NB - 1, :], x[(NB - 1) * P:N, :]).then_inc(s_ld[2], 16)
                q.wait_ge(s_ld[2], 32)

            @block.scalar
            def _(q):
                for f, a in enumerate((dst, src, etype)):
                    q.dma_start(ET1[0:ET - 1, f * P:(f + 1) * P], a[0:n_full].rearrange("(t e) -> t e", e=P)).then_inc(s_ld[3], 16)
                    q.dma_start(ET1[ET - 1:ET, f * P:f * P + TAIL], a[n_full:E].rearrange("(t e) -> t e", t=1)).then_inc(s_ld[3], 16)
                q.wait_ge(s_v, 2)
                for f in range(3):
                    q.dma_start(ET1[ET - 1:ET, f * P + TAIL:(f + 1) * P], TAILI[0:1, f * P + TAIL:(f + 1) * P]).then_inc(s_ld[3], 16)
                q.dma_start(MSG[E:EROWS, :], MTAIL[:, :]).then_inc(s_ld[4], 16)
                q.wait_ge(s_ld[4], 16)

            @block.gpsimd
            def _(q):
                c = Chain(q, s_pk)
                c.step(q.iota(IOTI[:, 0:P], pattern=[[1, P]], base=0, channel_multiplier=0))
                c.step(q.tensor_copy(IOTA[:], IOTI[:, 0:P]))
                c.step(q.iota(IOTI[:, 0:NB + 1], pattern=[[P, NB + 1]], base=0, channel_multiplier=0))
                c.step(q.tensor_copy(THR, IOTI[:, 0:NB + 1]))
                c.step(q.iota(IOTI[:, 0:1], pattern=[[0, 1]], base=0, channel_multiplier=1))
                c.step(q.tensor_copy(PCOL[:], IOTI[:, 0:1]))
                c.step(q.iota(IOTI[:, 0:SC], pattern=[[P, SC]], base=0, channel_multiplier=1))
                c.step(q.tensor_copy(ISTEP, IOTI[:, 0:SC]))
                c.step(q.iota(IOTI[:, 0:SW], pattern=[[1, SW]], base=0, channel_multiplier=0))
                c.step(q.tensor_copy(ITER, IOTI[:, 0:SW]))
                q.wait_ge(s_ld[3], 9 * 16)
                q.wait_ge(s_tix, 1)
                for col in range(SC):
                    if col >= 2:
                        q.wait_ge(s_tix, col)
                    q.indirect_dma_start(EGI[col % 2], None, ET1,
                                         bass.IndirectOffsetOnAxis(ap=TIX[:, col:col + 1], axis=0)).then_inc(s_eg, 16)
                    q.wait_ge(s_eg, 16 * (col + 1))

            @block.vector
            def _(q):
                q.memset(X[:, NB - 1, :], 0.0).then_inc(s_v, 1)
                c = Chain(q, s_k)
                c.inc(q.memset(MTAIL, 0.0))
                c.inc(q.memset(TAILI, 0))
                c.inc(q.memset(ONES[:], 1.0))
                c.hold()
                c.inc(q.memset(MTAIL[:, D + 1:D + 2], -FAR))
                c.inc(q.memset(TAILI[:, 0:P], -1))
                c.hold()
                q.sem_inc(s_v, 1)
                q.wait_ge(s_pk, 10)
                c.inc(q.tensor_scalar(IDENT[:], IOTA[:], PCOL[:], None, ALU.is_equal))
                c.inc(q.tensor_scalar(UST[:], IOTA[:], PCOL[:], None, ALU.is_gt))
                c.inc(q.tensor_scalar(USTB[:], IOTA[:], PCOL[:], None, ALU.is_gt))
                c.inc(q.tensor_scalar(LINB[:], IOTA[:], PCOL[:], None, ALU.is_le))
                for s, cnt in ((0, CNTA), (1, CNTB)):
                    q.wait_ge(s_ld[s], 16)
                    c.step(q.tensor_copy(EDF[0:EP, :], EDG[s][0:EP, :].bitcast(I32)))
                    with q.Fori(0, NB + 1) as b:
                        c.enter(b, 1)
                        c.inc(q.tensor_scalar(JUNK[0:EP, :], EDF[0:EP, :], THR[0:EP, bass.ds(b, 1)], 0.0,
                                              ALU.is_lt, ALU.add, accum_out=cnt[:, bass.ds(b, 1)]))
                        c.hold()
                        c.leave(NB + 1)
                pe = 0
                for s, (breg, treg) in enumerate(((BREGA, None), (BREGB, TREGB))):
                    q.sem_inc(s_v, 1)
                    pe += 1
                    q.wait_ge(s_pe, pe)
                    c.step(q.tensor_copy(SE, PS[0][0:NB, 0:2]))
                    start, end = SE[:, 0:1], SE[:, 1:2]
                    c.inc(q.tensor_copy(FL[:, 0:1], start))
                    c.inc(q.tensor_scalar(COL[:, 0:1], end, -1.0, None, ALU.add))
                    c.inc(q.tensor_tensor(COL[:, 1:2], end, start, ALU.is_gt))
                    c.hold()
                    c.step(q.tensor_copy(FL[:, 1:2], COL[:, 0:1]))
                    c.step(q.tensor_scalar(FL, FL, 7, None, ALU.arith_shift_right))
                    c.step(q.tensor_copy(COL[:, 2:4], FL))
                    c.step(q.tensor_tensor(COL[:, 4:5], COL[:, 3:4], COL[:, 2:3], ALU.subtract))
                    c.step(q.scalar_tensor_tensor(COL[:, 5:6], COL[:, 4:5], 1.0, COL[:, 1:2], ALU.add, ALU.mult))
                    q.sem_inc(s_v, 1)
                    pe += 1
                    q.wait_ge(s_pe, pe)
                    c.step(q.tensor_copy(COL[:, 6:7], PS[1][0:NB, 0:1]))
                    c.inc(q.tensor_tensor(COL[:, 7:8], COL[:, 6:7], COL[:, 5:6], ALU.add))
                    c.inc(q.tensor_tensor(RH[:, 1:2], COL[:, 2:3], COL[:, 6:7], ALU.subtract))
                    c.inc(q.tensor_scalar(RH[:, 0:1], PCOL[0:NB, :], float(-NB), None, ALU.add))
                    c.hold()
                    c.inc(q.tensor_scalar(BW[:, 0, :], ONES[0:NB, :], RH[:, 0:1], None, ALU.mult))
                    c.inc(q.tensor_scalar(BW[:, 1, :], ONES[0:NB, :], RH[:, 1:2], None, ALU.mult))
                    c.inc(q.tensor_scalar(TMPW[0:NB, :], ITER[0:NB, :], COL[:, 7:8], None, ALU.is_ge))
                    c.inc(q.tensor_scalar(SELX[0:NB, :], ITER[0:NB, :], COL[:, 6:7], None, ALU.is_ge))
                    c.hold()
                    c.step(q.tensor_tensor(SELX[0:NB, :], SELX[0:NB, :], TMPW[0:NB, :], ALU.subtract))
                    q.sem_inc(s_v, 1)
                    pe += 1
                    q.wait_ge(s_pe, pe)
                    bstep = SLOB[:] if s else DSTA[:]
                    for k in range(0, SW, 512):
                        w = min(512, SW - k)
                        c.inc(q.tensor_scalar(bstep[:, k:k + w], PS[2 + k // 512][:, 0:w], float(NB), None, ALU.add))
                    c.hold()
                    c.step(q.tensor_scalar(TMPW[0:1, :], bstep[0:1, :], float(NB - 1), None, ALU.min))
                    c.inc(q.tensor_copy(breg[:], TMPW[0:1, :]))
                    c.inc(q.tensor_scalar(bstep, bstep, float(P), None, ALU.mult))
                    c.hold()
                    q.sem_inc(s_v, 1)
                    pe += 1
                    q.wait_ge(s_pe, pe)
                    if s:
                        for k in range(0, SW, 512):
                            w = min(512, SW - k)
                            c.inc(q.tensor_tensor(TMPW[0:1, k:k + w], PS[2 + k // 512][0:1, 0:w], ITER[0:1, k:k + w], ALU.add))
                        c.hold()
                        c.step(q.tensor_scalar(TMPW[0:1, :], TMPW[0:1, :], float(ET - 1), None, ALU.min))
                        c.step(q.tensor_copy(treg[:], TMPW[0:1, :]))
                        continue
                    tl = PS[2][:, 0:SC]
                    c.step(q.tensor_tensor(TMPW[:, 0:SC], tl, ISTEP, ALU.add))
                    c.step(q.tensor_scalar(TMPW[:, 0:SC], TMPW[:, 0:SC], float(ET - 1), None, ALU.min))
                    c.step(q.tensor_copy(TIX, TMPW[:, 0:SC]))
                    q.sem_inc(s_tix, 1)
                    for col in range(SC):
                        q.wait_ge(s_eg, 16 * (col + 1))
                        c.step(q.tensor_copy(EGF, EGI[col % 2]))
                        q.sem_inc(s_tix, 1)
                        pe += 1
                        q.wait_ge(s_pe, pe)
                        at = slice(col * P, (col + 1) * P)
                        c.inc(q.tensor_tensor(DLOA[:, at], PS[6][:, 0:P], DSTA[:, at], ALU.subtract))
                        c.hold()
                        c.inc(q.tensor_copy(DSTA[:, at], PS[6][:, 0:P]))
                        c.inc(q.tensor_scalar(POSA[:, at], PS[6][:, P:2 * P], float(R), None, ALU.mult))
                        c.hold()
                        c.step(q.tensor_tensor(POSA[:, at], POSA[:, at], PS[6][:, 2 * P:3 * P], ALU.add))
                        c.step(q.tensor_copy(IDXA[:, at], POSA[:, at]))
                        q.sem_inc(s_v, 1)

            @block.tensor
            def _(q):
                v = 2
                for s, cnt in ((0, CNTA), (1, CNTB)):
                    v += 1
                    q.wait_ge(s_v, v)
                    q.matmul(PS[0][0:NB, 0:1], cnt[:, 0:NB], ONES[0:EP, 0:1], start=True, stop=True)
                    q.matmul(PS[0][0:NB, 1:2], cnt[:, 1:NB + 1], ONES[0:EP, 0:1], start=True, stop=True).then_inc(s_pe, 1)
                    v += 1
                    q.wait_ge(s_v, v)
                    q.matmul(PS[1][0:NB, 0:1], UST[0:NB, 0:NB], COL[:, 5:6], start=True, stop=True).then_inc(s_pe, 1)
                    v += 1
                    q.wait_ge(s_v, v)
                    for k in range(0, SW, 512):
                        w = min(512, SW - k)
                        last = q.matmul(PS[2 + k // 512][:, 0:w], BW[:, 0, :], SELX[0:NB, k:k + w], start=True, stop=True)
                    last.then_inc(s_pe, 1)
                    v += 1
                    q.wait_ge(s_v, v)
                    if s:
                        for k in range(0, SW, 512):
                            w = min(512, SW - k)
                            last = q.matmul(PS[2 + k // 512][:, 0:w], BW[:, 1, :], SELX[0:NB, k:k + w], start=True, stop=True)
                        last.then_inc(s_pe, 1)
                        continue
                    for col in range(SC):
                        last = q.matmul(PS[2][:, col:col + 1], SELX[0:NB, col * P:(col + 1) * P], RH[:, 1:2], start=True, stop=True)
                    last.then_inc(s_pe, 1)
                    for col in range(SC):
                        q.wait_ge(s_tix, col + 2)
                        for f in range(3):
                            last = q.transpose(PS[6][:, f * P:(f + 1) * P], EGF[:, f * P:(f + 1) * P], IDENT[:])
                        last.then_inc(s_pe, 1)
                        v += 1
                        q.wait_ge(s_v, v)
        XW = X[:].rearrange("p b d -> p (b d)")
        AD = ACC[:, :, 0:D]
        GW = G[:].rearrange("p r k w -> p (r k w)")
        HROWV = HROW.rearrange("(b p) w -> p b w", p=P)
        SIW, MJW = SI[:].rearrange("p b h -> p (b h)"), MJ[:].rearrange("p b h -> p (b h)")

        def wait(q, s, v):
            if not (isinstance(v, int) and v <= 0):
                q.wait_ge(s, v)

        def loop(q, times, body):
            body(0)
            with q.Fori(1, times) as j:
                body(j)

        def acc_of(reg, w):
            return words[:, bass.ds(reg * RW, w)]

        def blocks(q, breg, g, n=K, k0=0):
            return [q.value_load(breg[0:1, bass.ds(g * K + k0 + k, 1)], min_val=0, max_val=NB - 1) for k in range(n)]

        pool = [sem(f"work{i}") for i in range(20)]
        assert [s.num for s in pool] == list(range(pool[0].num, pool[0].num + len(pool)))
        in_use = [0]

        def own(name):
            in_use[0] += 1
            return pool[in_use[0] - 1]

        def fresh():
            if in_use[0]:
                with nc.Block() as block:
                    @block.sync
                    def _(q):
                        q.sem_clear(range(pool[0].num, pool[0].num + in_use[0]))
            in_use[0] = 0

        def norm_vector(q, c, s_var, s_std, s_norm):
            with q.Fori(0, NB // 2) as j:
                c.enter(j, 2)
                for u in range(2):
                    b = j * 2 + u
                    c.inc(q.bn_stats(ST6[:].rearrange("p b s -> p (b s)")[:, bass.ds(b * 6, 6)], XW[:, bass.ds(b * D, D)]))
                c.leave(NB // 2)
            c.hold()
            even, odd = ST6[:, :, 1], ST6[:, :, 4]
            c.inc(q.tensor_tensor(MV[:, :, 0], even, odd, ALU.add))
            c.inc(q.tensor_tensor(NMR[:], even, odd, ALU.subtract))
            c.inc(q.tensor_tensor(MV[:, :, 1], ST6[:, :, 2], ST6[:, :, 5], ALU.add))
            c.hold()
            c.inc(q.tensor_scalar(MV[:, :, 0], MV[:, :, 0], 0.5, None, ALU.mult))
            c.step(q.scalar_tensor_tensor(NMR[:], NMR[:], 0.25, NMR[:], ALU.mult, ALU.mult))
            c.step(q.scalar_tensor_tensor(MV[:, :, 1], MV[:, :, 1], 1.0 / D, NMR[:], ALU.mult, ALU.add))
            c.step(q.tensor_scalar(RSTD[:], MV[:, :, 1], LN_EPS, None, ALU.add))
            q.sem_inc(s_var, 1)
            q.wait_ge(s_std, 1)
            c.step(q.reciprocal(RSTD[:], RSTD[:]))
            c.step(q.scalar_tensor_tensor(NMR[:], MV[:, :, 0], -1.0, RSTD[:], ALU.mult, ALU.mult))
            q.sem_inc(s_norm, 1)

        def norm_scalar(q, s_var, s_std, s_norm):
            q.wait_ge(s_var, 1)
            q.activation(RSTD[:], RSTD[:], ACT.Sqrt).then_inc(s_std, 1)
            q.wait_ge(s_norm, 1)

        def dense(tag, normed, load, width, bias_at, table, before=None, prepare=None):
            fresh()
            s_w, s_var, s_std, s_norm, s_ch = own(tag + "w"), own(tag + "var"), own(tag + "std"), own(tag + "norm"), own(tag + "ch")
            s_h, s_tr, s_ht, s_mm, s_ea, s_ev = (own(tag + n) for n in ("h", "tr", "ht", "mm", "ea", "ev"))
            s_st = [own(tag + f"st{u}") for u in range(2)] if table else []
            s_o = own(tag + "o")
            tw = bias_at // 2
            stage = SCR[:].rearrange("p (u a) c -> p u (a c)", u=2)
            tabv = TAB.rearrange("(b p r) d -> p b (r d)", p=P, r=R)
            aw = width - bias_at
            evs = 2 if table or aw > RW else 1
            with nc.Block() as block:
                @block.sync
                def _(q):
                    n = load(q, s_w)
                    if table:
                        def body(j):
                            for u in range(2):
                                b = j * 2 + u
                                q.wait_ge(s_ea, b + 1)
                                q.wait_ge(s_ev, b * 2 + 1)
                                q.dma_start(tabv[:, bass.ds(b, 1), :], stage[:, u:u + 1, :]).then_inc(s_st[u], 16)
                        with q.Fori(0, NB // 2) as j:
                            body(j)
                        for s in s_st:
                            q.wait_ge(s, 16 * (NB // 2))
                    else:
                        q.wait_ge(s_ev, NB * evs)
                        q.dma_start(HROWV, ACC[:]).then_inc(s_o, 16)
                        q.wait_ge(s_o, 16)

                @block.scalar
                def _(q):
                    if normed:
                        norm_scalar(q, s_var, s_std, s_norm)

                    def body(j):
                        for u in range(2):
                            b = j * 2 + u
                            wait(q, s_tr, b - 1)
                            if normed:
                                q.activation(HB[:, u, :], XW[:, bass.ds(b * D, D)], ACT.Relu,
                                             bias=NMR[:, bass.ds(b, 1)], scale=RSTD[:, bass.ds(b, 1)]).then_inc(s_h, 1)
                            else:
                                q.activation(HB[:, u, :], words[:, bass.ds(b * RW, D)], ACT.Relu).then_inc(s_h, 1)
                            if table:
                                q.wait_ge(s_mm, b + 1)
                                wait(q, s_st[u], j * 16)
                                q.copy(stage[:, u, 0:tw], PS[2 + 3 * u][:, 0:tw]).then_inc(s_ea, 1)
                    loop(q, NB // 2, body)

                @block.vector
                def _(q):
                    c = Chain(q, s_ch)
                    if before:
                        before(q, c)
                    if normed:
                        norm_vector(q, c, s_var, s_std, s_norm)
                    if prepare:
                        prepare(q, c, s_w)
                        q.sem_inc(s_norm, 1)

                    def body(j):
                        for u in range(2):
                            b = j * 2 + u
                            q.wait_ge(s_tr, b + 1)
                            wait(q, s_mm, b - 1)
                            q.tensor_copy(HT[:, u, :], PS[u][:, 0:D]).then_inc(s_ht, 1)
                            q.wait_ge(s_mm, b + 1)
                            if table:
                                wait(q, s_st[u], j * 16)
                                q.tensor_copy(stage[:, u, tw:2 * tw], PS[3 + 3 * u][:, 0:tw]).then_inc(s_ev, 1)
                            if aw > RW:
                                q.tensor_tensor(SIW[:, bass.ds(b * 2 * HEADS, HEADS)], PS[4 + 3 * u][:, RW:aw], BIAS[:, RW:aw],
                                                ALU.add).then_inc(s_ev, 1)
                            q.tensor_tensor(words[:, bass.ds(b * RW, min(aw, RW))], PS[4 + 3 * u][:, 0:min(aw, RW)],
                                            BIAS[:, 0:min(aw, RW)], ALU.add).then_inc(s_ev, 1)
                    loop(q, NB // 2, body)

                @block.tensor
                def _(q):
                    if prepare:
                        q.wait_ge(s_norm, 2)
                    else:
                        q.wait_ge(s_w, load.total)

                    def body(j):
                        for u in range(2):
                            b = j * 2 + u
                            q.wait_ge(s_h, b + 1)
                            wait(q, s_ht, b - 1)
                            q.transpose(PS[u][:, 0:D], HB[:, u, :], IDENT[:]).then_inc(s_tr, 1)
                            q.wait_ge(s_ht, b + 1)
                            wait(q, s_ev, (b - 1) * evs)
                            if table:
                                wait(q, s_ea, b - 1)
                                q.matmul(PS[2 + 3 * u][:, 0:tw], HT[:, u, :], WT[:, 0:tw], start=True, stop=True)
                                q.matmul(PS[3 + 3 * u][:, 0:tw], HT[:, u, :], WT[:, tw:2 * tw], start=True, stop=True)
                            q.matmul(PS[4 + 3 * u][:, 0:aw], HT[:, u, :], WT[:, bias_at:width], start=True, stop=True).then_inc(s_mm, 1)
                    loop(q, NB // 2, body)

        def load_relations(W, wl, bias):
            def load(q, s):
                q.dma_start(WT[:, 0:R * D].rearrange("d (r h) -> d r h", r=R), W.rearrange("r d h -> d r h")).then_inc(s, 16)
                q.dma_start(WT[:, R * D:(R + 1) * D], wl).then_inc(s, 16)
                q.dma_start(BIAS[:, 0:D], bias.partition_broadcast(P)).then_inc(s, 16)
            load.total = 48
            return load

        def one_hot(q, r, dlo, g, op=ALU.is_equal):
            return q.tensor_tensor(OH[:, r % 2], bcast(IOTA[:].unsqueeze(1), P, K, P),
                                   bcast(dlo[:, bass.ds(g * K, K)].unsqueeze(2), P, K, P), op)

        def slot(k):
            return PS[k // 2][:, (k % 2) * 256:(k % 2) * 256 + RW]

        def groups(q, body):
            def ring(j):
                for r in range(RING):
                    body(j, r, j * RING + r)
            loop(q, NG // RING, ring)

        def add_half(q, s_mm, s_add, regs, g, h, w):
            wait(q, s_mm, 2 * g + h + 1)
            for k in range(K // 2):
                wait(q, s_add, g * K + h * K // 2 + k)
                a = acc_of(regs[k], w)
                q.tensor_tensor(a, a, slot(h * 4 + k)[:, 0:w], ALU.add).then_inc(s_add, 1)

        def gather(q, r, table, row, s_got):
            for k in range(K):
                q.indirect_dma_start(G[:, r, k, 0:row], None, table,
                                     bass.IndirectOffsetOnAxis(ap=IDS[:, r, k:k + 1], axis=0)).then_inc(s_got[r], 16)

        def sum_pass(tag, table, row, w, rank):
            fresh()
            s_ids, s_oh, s_mm, s_add = own(tag + "ids"), own(tag + "oh"), own(tag + "mm"), own(tag + "add")
            s_got = [sem(tag + f"got{r}") for r in range(RING)]
            s_cs, s_key, s_rk, s_pos, s_rc = (own(tag + n) for n in ("cs", "key", "rk", "pos", "rc")) if rank else [None] * 5
            KO = SCR[:].rearrange("p a c -> p (a c)").bitcast(BF16)[:, 0:2 * K * NB].rearrange("p (u k b) -> p u k b", u=2, k=K)
            RK = PS[4][:, 0:NB]
            with nc.Block() as block:
                @block.scalar
                def _(q):
                    def body(j, r, g):
                        wait(q, s_mm, 2 * (g - RING + 1))
                        q.copy(IDS[:, r, :], IDXA[:, bass.ds(g * K, K)]).then_inc(s_ids, 1)
                    groups(q, body)

                @block.gpsimd
                def _(q):
                    def body(j, r, g):
                        wait(q, s_ids, g + 1)
                        q.nop(nofuse=True)
                        gather(q, r, table, row, s_got)
                    groups(q, body)

                @block.vector
                def _(q):
                    if rank:
                        c = Chain(q, s_cs)

                    def keys(j, r, g):
                        at = bass.ds(g * K, K)
                        kbi = SM[:, 0, 0:K].bitcast(I32)
                        kb, below, inv = SM[:, 1, 0:K], SM[:, 2, 0:K], SM[:, 3 + r % 2, 0:K]
                        c.inc(q.tensor_scalar(kbi, IDXA[:, at], 10, None, ALU.arith_shift_right))
                        c.inc(q.tensor_scalar(below, DLOA[:, at], 0.0, None, ALU.is_lt))
                        c.hold()
                        c.inc(q.tensor_copy(kb, kbi))
                        c.inc(q.scalar_tensor_tensor(inv, DLOA[:, at], float(P - 1), below, ALU.is_gt, ALU.add))
                        c.hold()
                        c.step(q.scalar_tensor_tensor(kb, inv, 200.0, kb, ALU.mult, ALU.add))
                        q.tensor_tensor(KO[:, r % 2], bcast(IOTA[:, 0:NB].unsqueeze(1), P, K, NB),
                                        bcast(kb.unsqueeze(2), P, K, NB), ALU.is_equal).then_inc(s_key, 1)

                    def ranks(j, r, g, h):
                        for k in range(K // 2):
                            kk = h * 4 + k
                            q.wait_ge(s_rk, 2 * (g * K + kk) + 2)
                            q.tensor_tensor_reduce(out=HT[:, 0, 0:NB], in0=RK, in1=KO[:, r % 2, kk, :], scale=1.0, scalar=0.0,
                                                   op0=ALU.mult, op1=ALU.add, accum_out=SM[:, 5, kk:kk + 1]).then_inc(s_pos, 1)

                    def half(jr, h):
                        j, r, g = jr
                        regs = blocks(q, BREGA, g, K // 2, h * 4)
                        if rank:
                            ranks(j, r, g, h)
                        add_half(q, s_mm, s_add, regs, g, h, w)

                    def body(j, r, g):
                        wait(q, s_mm, 2 * (g - 1))
                        one_hot(q, r, DLOA, g).then_inc(s_oh, 1)
                        if rank:
                            keys(j, r, g)
                        half((j, r, g), 0)
                        half((j, r, g), 1)
                        if rank:
                            q.wait_ge(s_pos, (g + 1) * K)
                            c.step(q.scalar_tensor_tensor(POSA[:, bass.ds(g * K, K)], SM[:, 3 + r % 2, 0:K], FAR, SM[:, 5, 0:K],
                                                          ALU.mult, ALU.add))

                    def ring(j):
                        if rank:
                            c.enter(j, 6 * RING) if not isinstance(j, int) else None
                        for r in range(RING):
                            body(j, r, j * RING + r)
                    ring(0)
                    with q.Fori(1, NG // RING) as j:
                        if rank:
                            n0 = c.n
                            c.at, c.n = n0 * j, 0
                        for r in range(RING):
                            body(j, r, j * RING + r)
                        if rank:
                            assert c.n == n0

                @block.tensor
                def _(q):
                    if rank:
                        q.matmul(RK, ONES[0:EP, :], CNTB[:, 0:NB], start=True, stop=False, skip_group_check=True).then_inc(s_rk, 1)

                    def body(j, r, g):
                        q.wait_ge(s_got[r], 16 * K * (j + 1))
                        q.wait_ge(s_oh, g + 1)
                        if rank:
                            q.wait_ge(s_key, g + 1)
                        for h in range(2):
                            wait(q, s_add, (g - 1) * K + (h + 1) * K // 2)
                            for k in range(4):
                                kk = h * 4 + k
                                i = g * K + kk
                                if rank:
                                    q.matmul(RK, USTB[:], KO[:, r % 2, kk, :], start=False, stop=False, skip_group_check=True).then_inc(s_rk, 1)
                                m = q.matmul(slot(kk)[:, 0:w], OH[:, r % 2, kk, :], G[:, r, kk, 0:w], start=True, stop=True)
                                if k == 3:
                                    m.then_inc(s_mm, 1)
                                if rank:
                                    q.wait_ge(s_pos, i + 1)
                                    q.matmul(RK, LINB[:], KO[:, r % 2, kk, :], start=False, stop=False, skip_group_check=True).then_inc(s_rk, 1)
                    groups(q, body)
        def scatter_pass(tag):
            fresh()
            s_ids, s_oh, s_x, s_tr, s_ot, s_mm, s_cp, s_c = (own(tag + n) for n in ("ids", "oh", "x", "tr", "ot", "mm", "cp", "c"))
            s_sc = [sem(tag + f"sc{r}") for r in range(RING)]
            with nc.Block() as block:
                @block.scalar
                def _(q):
                    def body(j, r, g):
                        wait(q, s_sc[r], 16 * K * j)
                        q.copy(IDS[:, r, :], POSA[:, bass.ds(g * K, K)]).then_inc(s_ids, 1)
                        for h in range(2):
                            q.wait_ge(s_tr, 2 * g + h + 1)
                            wait(q, s_mm, 2 * g + h - 1)
                            q.copy(SCR[:, h, :], PS[4 + h][:]).then_inc(s_ot, 1)
                    groups(q, body)

                @block.vector
                def _(q):
                    c = Chain(q, s_c)
                    c.step(q.memset(GW, 0.0))
                    c.step(q.memset(G[:, :, :, D:D + 1], 1.0))

                    def body(j, r, g):
                        wait(q, s_tr, 2 * (g - 1))
                        one_hot(q, r, DLOA, g).then_inc(s_oh, 1)
                        wait(q, s_sc[r], 16 * K * j)
                        srci = SM[:, r, 0:K].bitcast(I32)
                        q.tensor_scalar(srci, IDXA[:, bass.ds(g * K, K)], 3, None, ALU.arith_shift_right).then_inc(s_x, 1)
                        q.tensor_copy(G[:, r, :, D + 2], DSTA[:, bass.ds(g * K, K)]).then_inc(s_x, 1)
                        q.wait_ge(s_x, 3 * g + 2)
                        q.tensor_copy(G[:, r, :, D + 1], srci).then_inc(s_x, 1)
                        for h in range(2):
                            q.wait_ge(s_mm, 2 * g + h + 1)
                            for n in range(2):
                                q.tensor_copy(G[:, r, h * 4 + 2 * n:h * 4 + 2 * n + 2, 0:D],
                                              PS[2 * h + n][:].rearrange("p (s w) -> p s w", s=2)[:, :, 0:D]).then_inc(s_cp, 1)
                    groups(q, body)

                @block.tensor
                def _(q):
                    def body(j, r, g):
                        regs = blocks(q, BREGA, g)
                        q.wait_ge(s_oh, g + 1)
                        for h in range(2):
                            wait(q, s_ot, 2 * g + h - 1)
                            for k in range(4):
                                m = q.transpose(PS[4 + h][:, k * P:(k + 1) * P], OH[:, r % 2, h * 4 + k, :], IDENT[:])
                            m.then_inc(s_tr, 1)
                        for h in range(2):
                            q.wait_ge(s_ot, 2 * g + h + 1)
                            wait(q, s_cp, 4 * (g - 1) + 2 * h + 2)
                            for k in range(4):
                                m = q.matmul(slot(h * 4 + k)[:, 0:D], SCR[:, h, k * P:(k + 1) * P], acc_of(regs[h * 4 + k], D),
                                             start=True, stop=True)
                            m.then_inc(s_mm, 1)
                    groups(q, body)

                @block.gpsimd
                def _(q):
                    def body(j, r, g):
                        q.wait_ge(s_ids, g + 1)
                        q.wait_ge(s_x, 3 * g + 3)
                        q.wait_ge(s_cp, 4 * g + 4)
                        q.nop(nofuse=True)
                        for k in range(K):
                            q.indirect_dma_start(MSG, bass.IndirectOffsetOnAxis(ap=IDS[:, r, k:k + 1], axis=0), G[:, r, k, :], None,
                                                 bounds_check=E - 1, oob_is_err=False).then_inc(s_sc[r], 16)
                    groups(q, body)
                    for s in s_sc:
                        q.wait_ge(s, 16 * K * (NG // RING))

        def message_pass(tag, w):
            fresh()
            s_oh, s_mm, s_add, s_c = (own(tag + n) for n in ("oh", "mm", "add", "c"))
            s_got = [own(tag + f"got{r}") for r in range(RING)]
            tiles = MSG.rearrange("(t p) w -> t p w", p=P)
            with nc.Block() as block:
                def load(q, parity):
                    def body(j, r, g):
                        if r % 2 != parity:
                            return
                        regs = [q.value_load(TREGB[0:1, bass.ds(g * K + k, 1)], min_val=0, max_val=ET - 1) for k in range(K)]
                        wait(q, s_mm, 2 * (g - RING + 1))
                        wait(q, s_oh, g - RING + 1)
                        for k in range(K):
                            q.dma_start(G[:, r, k, :], tiles[bass.ds(regs[k], 1), :, :].rearrange("o p w -> p (o w)")).then_inc(s_got[r], 16)
                    groups(q, body)

                @block.sync
                def _(q):
                    load(q, 0)

                @block.scalar
                def _(q):
                    load(q, 1)

                @block.vector
                def _(q):
                    c = Chain(q, s_c)
                    c.step(q.memset(words, 0.0))
                    n0 = c.n

                    def body(j, r, g):
                        regs = blocks(q, BREGB, g)
                        q.wait_ge(s_got[r], 16 * K * (j + 1))
                        at = bass.ds(g * K, K)
                        q.tensor_copy(IDXB[:, at], G[:, r, :, D + 2]).then_inc(s_c, 1)
                        q.tensor_tensor(SLOB[:, at], G[:, r, :, D + 1], SLOB[:, at], ALU.subtract).then_inc(s_c, 1)
                        q.wait_ge(s_c, n0 + 2 * g + 2)
                        wait(q, s_mm, 2 * (g - 1))
                        one_hot(q, r, SLOB, g).then_inc(s_oh, 1)
                        for h in range(2):
                            add_half(q, s_mm, s_add, regs[h * 4:h * 4 + 4], g, h, w)
                    groups(q, body)

                @block.tensor
                def _(q):
                    sums(q, s_got, s_oh, s_add, s_mm, w)

        def sums(q, s_got, s_oh, s_add, s_mm, w):
            def body(j, r, g):
                q.wait_ge(s_got[r], 16 * K * (j + 1))
                q.wait_ge(s_oh, g + 1)
                for h in range(2):
                    wait(q, s_add, (g - 1) * K + (h + 1) * K // 2)
                    for k in range(h * 4, h * 4 + 4):
                        m = q.matmul(slot(k)[:, 0:w], OH[:, r % 2, k, :], G[:, r, k, 0:w], start=True, stop=True)
                    m.then_inc(s_mm, 1)
            groups(q, body)

        STG = [GW[:, i * CH * D:(i + 1) * CH * D].rearrange("p (b d) -> p b d", b=CH) for i in range(2)]

        def load_rows(q, s_row, s_use):
            for n in range(NCH):
                wait(q, s_use, n - 1)
                q.dma_start(STG[n % 2], HROWV[:, n * CH:(n + 1) * CH, 0:D]).then_inc(s_row[n % 2], 16)

        def batch_norm_stage(tag):
            fresh()
            s_row, s_use, s_p, s_c, s_m, s_sq, s_pe, s_g = ([own(tag + "row0"), own(tag + "row1")], own(tag + "use"), own(tag + "p"),
                                                            own(tag + "c"), own(tag + "m"), own(tag + "sq"), own(tag + "pe"), own(tag + "g"))
            MEAN, VAR, GAM, BET = HB[:, 0, :], HB[:, 1, :], HT[:, 0, :], HT[:, 1, :]

            def node_sums(q, rows, blocks_of, first, last):
                b = 0
                while b < len(blocks_of):
                    n = min(4, len(blocks_of) - b)
                    if blocks_of[b + n - 1] == NB - 1 and n > 1:
                        n -= 1
                    k = LAST if blocks_of[b] == NB - 1 else P
                    m = q.matmul(PS[0][:, 0:n * D], ONES[0:k, :], rows[0:k, b:b + n, :], start=first and b == 0,
                                 stop=last and b + n == len(blocks_of), skip_group_check=True)
                    b += n
                return m

            with nc.Block() as block:
                @block.sync
                def _(q):
                    q.dma_start(GAM, gamma.partition_broadcast(P)).then_inc(s_g, 16)
                    q.dma_start(BET, beta.partition_broadcast(P)).then_inc(s_g, 16)
                    load_rows(q, s_row, s_use)

                @block.vector
                def _(q):
                    c = Chain(q, s_c)
                    cnt = MV[:, :, 0]
                    c.step(q.tensor_scalar(cnt, ACC[:, :, D], 1e-8, None, ALU.add))
                    c.step(q.reciprocal(cnt, cnt))
                    c.step(q.tensor_tensor(AD, AD, bcast(cnt.unsqueeze(2), P, NB, D), ALU.mult))
                    for n in range(NCH):
                        q.wait_ge(s_row[n % 2], 16 * (n // 2 + 1))
                        a = ACC[:, n * CH:(n + 1) * CH, 0:D]
                        q.tensor_tensor(a, a, STG[n % 2], ALU.add).then_inc(s_use, 1)
                    q.wait_ge(s_pe, 1)
                    for t, at in ((MEAN, 1), (VAR, 2)):
                        q.wait_ge(s_pe, at)
                        c.step(q.tensor_reduce(t, PS[0][:].rearrange("p (s d) -> p d s", s=4), AX.X, ALU.add))
                        c.step(q.tensor_scalar(t, t, 1.0 / N, None, ALU.mult))
                        if at == 1:
                            q.tensor_tensor(AD, AD, bcast(MEAN.unsqueeze(1), P, NB, D), ALU.subtract).then_inc(s_m, 1)
                    c.step(q.tensor_scalar(VAR, VAR, BN_EPS, None, ALU.add))
                    q.sem_inc(s_p, 1)
                    q.wait_ge(s_sq, NCH + 1)
                    c.step(q.reciprocal(VAR, VAR))
                    q.wait_ge(s_g, 32)
                    c.step(q.tensor_tensor(GAM, GAM, VAR, ALU.mult))
                    c.step(q.tensor_tensor(AD, AD, bcast(GAM.unsqueeze(1), P, NB, D), ALU.mult))
                    c.step(q.tensor_tensor(AD, AD, bcast(BET.unsqueeze(1), P, NB, D), ALU.add))

                @block.tensor
                def _(q):
                    q.wait_ge(s_use, NCH)
                    node_sums(q, AD, list(range(NB)), True, True).then_inc(s_pe, 1)
                    for n in range(NCH):
                        q.wait_ge(s_sq, n + 1)
                        m = node_sums(q, STG[n % 2], list(range(n * CH, (n + 1) * CH)), n == 0, n == NCH - 1)
                        m.then_inc(s_use, 1)
                    q.sem_inc(s_use, 1)
                    m = q.matmul(PS[1][:, 0:1], ONES[:], ONES[:, 0:1], start=True, stop=True)
                    m.then_inc(s_pe, 1)

                @block.scalar
                def _(q):
                    q.wait_ge(s_m, 1)
                    for n in range(NCH):
                        if n >= 2:
                            q.wait_ge(s_use, NCH + n - 1)
                        q.activation(STG[n % 2], ACC[:, n * CH:(n + 1) * CH, 0:D], ACT.Square).then_inc(s_sq, 1)
                    q.wait_ge(s_p, 1)
                    q.activation(VAR, VAR, ACT.Sqrt).then_inc(s_sq, 1)

        def largest_pass(tag):
            fresh()
            s_ids, s_oh, s_v, s_tr, s_red, s_mx, s_c = (own(tag + n) for n in ("ids", "oh", "v", "tr", "red", "mx", "c"))
            s_got, s_st = [sem(tag + f"got{r}") for r in range(RING)], [own(tag + f"st{r}") for r in range(RING)]
            keep = KEEP.rearrange("g p w -> p g w")
            with nc.Block() as block:
                @block.sync
                def _(q):
                    def body(j, r, g):
                        q.wait_ge(s_got[r], 16 * K * (j + 1))
                        q.dma_start(keep[:, bass.ds(g, 1), :], G[:, r, :, :].rearrange("p k w -> p (k w)").unsqueeze(1)).then_inc(s_st[r], 16)
                    groups(q, body)
                    for s in s_st:
                        q.wait_ge(s, 16 * (NG // RING))

                @block.gpsimd
                def _(q):
                    def body(j, r, g):
                        q.wait_ge(s_ids, g + 1)
                        wait(q, s_st[r], 16 * j)
                        wait(q, s_v, (g - RING + 1) * K)
                        q.nop(nofuse=True)
                        gather(q, r, HROW, RW, s_got)
                    groups(q, body)

                @block.scalar
                def _(q):
                    def body(j, r, g):
                        wait(q, s_got[r], 16 * K * j)
                        q.copy(IDS[:, r, :], IDXB[:, bass.ds(g * K, K)]).then_inc(s_ids, 1)

                    def scores(j, r, g):
                        q.wait_ge(s_got[r], 16 * K * (j + 1))
                        q.wait_ge(s_oh, g + 1)
                        for k in range(K):
                            wait(q, s_tr, g * K + k - 3)
                            for hd in range(HEADS):
                                m = q.activation(SCR[:, k % 4, hd * P:(hd + 1) * P], OH[:, r % 2, k, :], ACT.Identity,
                                                 bias=G[:, r, k, D + hd:D + hd + 1], scale=-BIG)
                            m.then_inc(s_v, 1)

                    def ring(j):
                        for r in range(RING):
                            body(j, r, j * RING + r)
                        for r in range(RING):
                            scores(j, r, j * RING + r)
                    loop(q, NG // RING, ring)

                @block.tensor
                def _(q):
                    def body(j, r, g):
                        for k in range(K):
                            q.wait_ge(s_v, g * K + k + 1)
                            wait(q, s_red, (g - 1) * K + k + 1)
                            for hd in range(HEADS):
                                m = q.transpose(PS[k][:, hd * P:(hd + 1) * P], SCR[:, k % 4, hd * P:(hd + 1) * P], IDENT[:])
                            m.then_inc(s_tr, 1)
                    groups(q, body)

                @block.vector
                def _(q):
                    c = Chain(q, s_c)
                    c.inc(q.memset(MJ[:], -BIG))
                    c.step(q.memset(words, 0.0))
                    n0 = c.n

                    def body(j, r, g):
                        regs = blocks(q, BREGB, g)
                        wait(q, s_v, K * (g - 1))
                        one_hot(q, r, SLOB, g, ALU.not_equal).then_inc(s_oh, 1)
                        for k in range(K):
                            q.wait_ge(s_tr, g * K + k + 1)
                            t = SM[:, 0, k * HEADS:(k + 1) * HEADS]
                            wait(q, s_mx, (g - 1) * K + k + 1)
                            q.tensor_reduce(t, PS[k][:].rearrange("p (h e) -> p h e", h=HEADS), AX.X, ALU.max).then_inc(s_red, 1)
                            q.wait_ge(s_red, g * K + k + 1)
                            wait(q, s_mx, g * K + k)
                            a = MJW[:, bass.ds(regs[k] * HEADS, HEADS)]
                            q.tensor_tensor(a, a, t, ALU.max).then_inc(s_mx, 1)
                    groups(q, body)

        def attention_pass(tag):
            fresh()
            s_got = [own(tag + f"got{r}") for r in range(RING)]
            s_c, s_oh, s_tr, s_ot, s_sc, s_z, s_ex, s_wt, s_mm, s_add = (own(tag + n) for n in ("c", "oh", "tr", "ot", "sc", "z", "ex", "wt", "mm", "add"))
            keep = KEEP.rearrange("g p w -> p g w")

            def scores_of(r):
                return PS[6 + r % 2][:, 0:K * 2 * HEADS].rearrange("p (k h) -> p k h", k=K)

            def z_of(r):
                return SM[:, r % 2, :].rearrange("p (k h) -> p k h", k=K)

            with nc.Block() as block:
                @block.sync
                def _(q):
                    def body(j, r, g):
                        wait(q, s_mm, 2 * (g - RING + 1))
                        q.dma_start(G[:, r, :, :].rearrange("p k w -> p (k w)").unsqueeze(1), keep[:, bass.ds(g, 1), :]).then_inc(s_got[r], 16)
                    groups(q, body)

                @block.vector
                def _(q):
                    c = Chain(q, s_c)
                    mi = SI[:, :, HEADS:2 * HEADS]
                    c.step(q.tensor_tensor(mi, SI[:, :, 0:HEADS], MJ[:], ALU.add))
                    c.step(q.scalar_tensor_tensor(mi, mi, SLOPE, mi, ALU.mult, ALU.max))
                    n0 = c.n

                    def weights(j, r, g):
                        z = z_of(r)
                        q.wait_ge(s_sc, g + 1)
                        q.wait_ge(s_got[r], 16 * (j + 1))
                        wait(q, s_wt, 2 * (g - 1))
                        q.tensor_tensor(z, scores_of(r)[:, :, 0:HEADS], G[:, r, :, D:RW], ALU.add).then_inc(s_z, 1)
                        q.wait_ge(s_z, 4 * g + 1)
                        q.scalar_tensor_tensor(z, z, SLOPE, z, ALU.mult, ALU.max).then_inc(s_z, 1)
                        q.wait_ge(s_z, 4 * g + 2)
                        q.tensor_tensor(z, z, scores_of(r)[:, :, HEADS:2 * HEADS], ALU.subtract).then_inc(s_z, 1)
                        q.wait_ge(s_z, 4 * g + 3)
                        q.tensor_scalar(z, z, 0.0, None, ALU.min).then_inc(s_z, 1)

                    def weigh(j, r, g):
                        q.wait_ge(s_ex, g + 1)
                        z = z_of(r)
                        rows = G[:, r, :, 0:D].rearrange("p k (h f) -> p k h f", h=HEADS)
                        q.tensor_tensor(rows, rows, bcast(z.unsqueeze(3), P, K, HEADS, HD), ALU.mult).then_inc(s_wt, 1)
                        q.tensor_copy(G[:, r, :, D:RW], z).then_inc(s_wt, 1)

                    def body(j, r, g):
                        wait(q, s_mm, 2 * (g - 1))
                        one_hot(q, r, SLOB, g).then_inc(s_oh, 1)
                        weights(j, r, g)
                        regs = blocks(q, BREGB, g)
                        weigh(j, r, g)
                        for h in range(2):
                            add_half(q, s_mm, s_add, regs[h * 4:h * 4 + 4], g, h, RW)
                    groups(q, body)

                @block.scalar
                def _(q):
                    def body(j, r, g):
                        for h in range(2):
                            q.wait_ge(s_tr, 2 * g + h + 1)
                            wait(q, s_sc, g)
                            q.copy(SCR[:, h, :], PS[4 + h][:]).then_inc(s_ot, 1)
                        q.wait_ge(s_z, 4 * g + 4)
                        q.activation(z_of(r), z_of(r), ACT.Exp).then_inc(s_ex, 1)
                    groups(q, body)

                @block.tensor
                def _(q):
                    q.wait_ge(s_c, 2)
                    def body(j, r, g):
                        regs = blocks(q, BREGB, g)
                        q.wait_ge(s_oh, g + 1)
                        for h in range(2):
                            wait(q, s_ot, 2 * g + h - 1)
                            for k in range(4):
                                m = q.transpose(PS[4 + h][:, k * P:(k + 1) * P], OH[:, r % 2, h * 4 + k, :], IDENT[:])
                            m.then_inc(s_tr, 1)
                        wait(q, s_z, 4 * (g - 1) - 1)
                        for h in range(2):
                            q.wait_ge(s_ot, 2 * g + h + 1)
                            for k in range(4):
                                m = q.matmul(scores_of(r)[:, h * 4 + k, :], SCR[:, h, k * P:(k + 1) * P],
                                             SIW[:, bass.ds(regs[h * 4 + k] * 2 * HEADS, 2 * HEADS)], start=True, stop=True)
                        m.then_inc(s_sc, 1)
                        q.wait_ge(s_wt, 2 * g + 2)
                        for h in range(2):
                            wait(q, s_add, (g - 1) * K + (h + 1) * K // 2)
                            for k in range(h * 4, h * 4 + 4):
                                m = q.matmul(slot(k), OH[:, r % 2, k, :], G[:, r, k, :], start=True, stop=True)
                            m.then_inc(s_mm, 1)
                    groups(q, body)

        dense("d0", True, load_relations(W1, loop1, b1), (R + 1) * D, R * D, True)
        sum_pass("g0", TAB, D, D, True)
        dense("d1", False, load_relations(W2, loop2, b2), (R + 1) * D, R * D, True)
        sum_pass("g1", TAB, D, D, False)

        def load_square(W, bias, more=None):
            def load(q, s):
                q.dma_start(WT[:, 0:D], W).then_inc(s, 16)
                q.dma_start(BIAS[:, 0:D], bias.partition_broadcast(P)).then_inc(s, 16)
                if more is not None:
                    q.dma_start(GW[:, 0:2 * D], more.rearrange("a h f -> (a h f)").partition_broadcast(P)).then_inc(s, 16)
            load.total = 48 if more is not None else 32
            return load

        def add_to_x(q, c):
            c.step(q.tensor_tensor(X[:], X[:], AD, ALU.add))
            c.step(q.memset(ACC[:, :, D:RW], 0.0))

        dense("d2", True, load_square(lw, lb), D, 0, False, before=add_to_x)
        scatter_pass("sc")
        message_pass("ms", D + 1)
        batch_norm_stage("bn")
        def project_attention(q, c, s_w):
            q.wait_ge(s_w, 48)
            a = GW[:, 0:2 * D].rearrange("p (h f) -> p h f", h=HEADS)
            t = GW[:, 2 * D:3 * D].rearrange("p (h f) -> p h f", h=HEADS)
            for m in (WT, BIAS):
                for at, f0 in ((D, HD), (RW, 0)):
                    c.step(q.tensor_tensor(t, m[:, 0:D].rearrange("p (h f) -> p h f", h=HEADS), a[:, :, f0:f0 + HD], ALU.mult))
                    c.step(q.tensor_reduce(m[:, at:at + HEADS], t, AX.X, ALU.add))

        dense("d3", True, load_square(gw, gb, attn), RW + HEADS, 0, False, before=lambda q, c: c.step(q.tensor_tensor(X[:], X[:], AD, ALU.add)),
              prepare=project_attention)
        largest_pass("lp")
        attention_pass("at")
        fresh()
        s_row, s_use, s_c, s_var, s_std, s_norm, s_h, s_o = ([own("f_row0"), own("f_row1")], own("f_use"), own("f_c"), own("f_var"), own("f_std"),
                                                             own("f_norm"), own("f_h"), own("f_o"))
        with nc.Block() as block:
            @block.sync
            def _(q):
                load_rows(q, s_row, s_use)
                q.wait_ge(s_h, 1 + NB)
                q.dma_start(HROWV, ACC[:]).then_inc(s_o, 16)
                q.wait_ge(s_o, 16)

            @block.vector
            def _(q):
                c = Chain(q, s_c)
                den = MJ[:]
                c.step(q.tensor_scalar(den, ACC[:, :, D:RW], 1e-30, None, ALU.max))
                c.step(q.reciprocal(den, den))
                sums4 = AD.rearrange("p b (h f) -> p b h f", h=HEADS)
                c.step(q.tensor_tensor(sums4, sums4, bcast(den.unsqueeze(3), P, NB, HEADS, HD), ALU.mult))
                c.step(q.tensor_tensor(X[:], X[:], AD, ALU.add))
                for n in range(NCH):
                    q.wait_ge(s_row[n % 2], 16 * (n // 2 + 1))
                    a = X[:, n * CH:(n + 1) * CH, :]
                    q.tensor_tensor(a, a, STG[n % 2], ALU.add).then_inc(s_use, 1)
                q.wait_ge(s_use, NCH)
                norm_vector(q, c, s_var, s_std, s_norm)
                c.inc(q.memset(ACC[:, :, D + 1:RW], 0.0))
                c.inc(q.memset(ACC[:, :, D:D + 1], 1.0))
                c.inc(q.tensor_scalar(IDXA[:], IDXA[:], 3, None, ALU.arith_shift_right))
                c.hold()
                q.sem_inc(s_h, 1)

            @block.scalar
            def _(q):
                norm_scalar(q, s_var, s_std, s_norm)
                with q.Fori(0, NB) as b:
                    q.activation(words[:, bass.ds(b * RW, D)], XW[:, bass.ds(b * D, D)], ACT.Relu,
                                 bias=NMR[:, bass.ds(b, 1)], scale=RSTD[:, bass.ds(b, 1)]).then_inc(s_h, 1)
        with nc.Block() as block:
            s_z = own("f_z")

            @block.vector
            def _(q):
                q.memset(words, 0.0).then_inc(s_z, 1)
        sum_pass("g3", HROW, RW, D + 1, False)
        fresh()
        s_c, s_f, s_o = own("e_c"), own("e_f"), own("e_o")
        with nc.Block() as block:
            @block.vector
            def _(q):
                c = Chain(q, s_c)
                cnt = MV[:, :, 0]
                c.step(q.tensor_scalar(cnt, ACC[:, :, D], 1.0, None, ALU.max))
                c.step(q.reciprocal(cnt, cnt))
                c.step(q.tensor_tensor(AD, AD, bcast(cnt.unsqueeze(2), P, NB, D), ALU.mult))
                q.tensor_tensor(X[:], X[:], AD, ALU.add).then_inc(s_f, 1)

            @block.sync
            def _(q):
                q.wait_ge(s_f, 1)
                q.dma_start(out[0:(NB - 1) * P, :].rearrange("(b p) d -> p b d", p=P), X[:, 0:NB - 1, :]).then_inc(s_o, 16)
                q.dma_start(out[(NB - 1) * P:N, :], X[0:LAST, NB - 1, :]).then_inc(s_o, 16)
                q.wait_ge(s_o, 32)


_INS = ['x', 'src', 'dst', 'edge_type_8', 'L0_gnn_W1', 'L0_gnn_loop1', 'L0_gnn_b1', 'L0_gnn_W2', 'L0_gnn_loop2',
        'L0_gnn_b2', 'L1_gnn_W', 'L1_gnn_b', 'L1_gnn_gamma', 'L1_gnn_beta', 'L2_gnn_W', 'L2_gnn_b', 'L2_gnn_attn']


def kernel(**inputs):
    import numpy as np
    import concourse.bacc as bacc
    from concourse.bass_utils import run_bass_kernel_spmd

    nc = bacc.Bacc("TRN2", target_bir_lowering=False, num_devices=1)
    arrays, args = {}, []
    for name in _INS:
        a = np.asarray(inputs[name])
        if name == 'L1_gnn_W':
            a = a.T
        arrays[f"in_{name}"] = a = np.ascontiguousarray(a)
        args.append(nc.dram_tensor(f"in_{name}", a.shape, mybir.dt.from_np(a.dtype), kind="ExternalInput").ap())
    out = nc.dram_tensor("out", (N, D), F32, kind="ExternalOutput").ap()
    build_gnn(nc, *args, out)
    return run_bass_kernel_spmd(nc, [arrays], core_ids=[0]).results[0]["out"]
```

```python
import concourse.bass as bass
from concourse import mybir
from contextlib import ExitStack

F32, I32, BF16 = mybir.dt.float32, mybir.dt.int32, mybir.dt.bfloat16
ALU = mybir.AluOpType
ACT = mybir.ActivationFunctionType
AX = mybir.AxisListType

P = 128
N, D, E, R = 12500, 128, 212500, 8
HEADS, HD = 4, 32
NB = -(-N // P)
LAST = N - (NB - 1) * P
ET = -(-E // P)
TAIL = E - (ET - 1) * P
EP = 125
EC = E // EP
K = 8
RING = 4
MAX_STEPS = ET + NB - 1
NG = -(-MAX_STEPS // (K * RING)) * RING
NS = NG * K
SC = -(-NS // P)
SW = SC * P
RW = D + HEADS
ROWS = NB * P
EROWS = ET * P
LN_EPS = BN_EPS = 1e-5
SLOPE = 0.2
BIG = 1e30
FAR = float(1 << 20)
CH = 14
NCH = NB // CH


class Chain:

    def __init__(self, eng, sem):
        self.eng, self.sem, self.n, self.at = eng, sem, 0, 0

    def inc(self, ins):
        ins.then_inc(self.sem, 1)
        self.n += 1
        return ins

    def hold(self):
        self.eng.wait_ge(self.sem, self.at + self.n)

    def step(self, ins):
        self.inc(ins)
        self.hold()

    def enter(self, i, per):
        self.outer, self.per = self.n, per
        self.at, self.n = self.outer + i * per, 0

    def leave(self, times):
        assert self.n == self.per, (self.n, self.per)
        self.n, self.at = self.outer + times * self.per, 0


def build_gnn(nc, x, src, dst, etype, W1, loop1, b1, W2, loop2, b2, lw, lb, gamma, beta, gw, gb, attn, out):
    ctx = ExitStack()
    sb = lambda name, shape, dt=F32: ctx.enter_context(nc.sbuf_tensor(name, shape, dt))
    sem = lambda name: ctx.enter_context(nc.semaphore(name))
    dram = lambda name, shape, dt=F32: nc.dram_tensor(name, shape, dt, kind="Internal").ap()

    with ctx:
        X = sb("X", [P, NB, D])
        ACC = sb("ACC", [P, NB, RW])
        IDXA = sb("IDXA", [P, SW], I32)
        DLOA = sb("DLOA", [P, SW])
        DSTA = sb("DSTA", [P, SW])
        POSA = sb("POSA", [P, SW])
        IDXB = DSTA[:].bitcast(I32)
        SLOB = sb("SLOB", [P, SW])
        BREGA = sb("BREGA", [1, SW], I32)
        BREGB = sb("BREGB", [1, SW], I32)
        TREGB = sb("TREGB", [1, SW], I32)
        G = sb("G", [P, RING, K, RW])
        OH = sb("OH", [P, 2, K, P])
        IDS = sb("IDS", [P, RING, K], I32)
        WT = sb("WT", [P, (R + 1) * D])
        BIAS = sb("BIAS", [P, RW + HEADS])
        IOTA = sb("IOTA", [P, P])
        PCOL = sb("PCOL", [P, 1])
        IDENT = sb("IDENT", [P, P])
        UST = sb("UST", [P, P])
        USTB = sb("USTB", [P, P], BF16)
        LINB = sb("LINB", [P, P], BF16)
        ONES = sb("ONES", [P, P])
        CNTB = sb("CNTB", [EP, NB + 1])
        ST6 = sb("ST6", [P, NB, 6])
        MV = sb("MV", [P, NB, 2])
        RSTD, NMR = sb("RSTD", [P, NB]), sb("NMR", [P, NB])
        SCR = sb("SCR", [P, 4, 4 * P])
        HB, HT = sb("HB", [P, 2, D]), sb("HT", [P, 2, D])
        SM = sb("SM", [P, 6, K * HEADS])
        SI = sb("SI", [P, NB, 2 * HEADS])
        MJ = sb("MJ", [P, NB, HEADS])
        PSUM = ctx.enter_context(nc.psum_tensor("PSUM", [P, 8 * 512], F32))
        PS = [PSUM[:, i * 512:(i + 1) * 512] for i in range(8)]
        TAB = dram("TAB", [ROWS * R, D])
        HROW = dram("HROW", [ROWS, RW])
        ET1 = dram("ET1", [ET, 3 * P], I32)
        ET2 = dram("ET2", [ET, 3 * P], I32)
        MSG = dram("MSG", [EROWS, RW])
        KEEP = dram("KEEP", [NG, P, K * RW])

        def bcast(ap, *shape):
            return ap.broadcast_to(list(shape))

        words = ACC[:].rearrange("p b w -> p (b w)")
        used = [0]

        def part(n):
            a = words[:, used[0]:used[0] + n]
            used[0] += n
            return a

        s_ld = [sem(f"s_ld{i}") for i in range(6)]
        s_bad, chains = sem("s_bad"), []
        s_k, s_pk, s_v = sem("s_k"), sem("s_pk"), sem("s_v")
        s_pe, s_eg, s_tix = sem("s_pe"), sem("s_eg"), sem("s_tix")
        EDG = [part(EC), part(EC)]
        EDF = part(EC)
        SELX, ITER, TMPW = part(SW), part(SW), part(SW)
        EGI = [part(3 * P).bitcast(I32) for _ in range(2)]
        EGF = part(3 * P)
        JUNK = OH[:].rearrange("p a k n -> p (a k n)")[:, 0:EC]
        JUNKS = [JUNK, POSA[:, 0:EC], DLOA[:, 0:EC]]
        SIGNS = [a.bitcast(BF16)[:, 0:EC] for a in (SLOB[:, 0:SW // 2], SLOB[:, SW // 2:SW], DSTA[:, 0:SW // 2])]
        SRCF = IDXA[:, 0:EC].bitcast(F32)
        assert (NB + 1) % len(JUNKS) == 0
        IOTI = G[:].rearrange("p r k w -> p (r k w)")[:, 0:SW].bitcast(I32)
        small = SCR[:].rearrange("p a c -> p (a c)")
        taken = [0]

        def cut(rows, n):
            a = small[0:rows, taken[0]:taken[0] + n]
            taken[0] += n
            return a

        NTHR, s_cnt = cut(P, NB + 1), sem("s_cnt")
        THR, CNTA, ISTEP = cut(P, NB + 1), cut(EP, NB + 1), cut(P, SC)
        SE, FL, COL, RH = cut(NB, 2), cut(NB, 2).bitcast(I32), cut(NB, 8), cut(NB, 2)
        BW = cut(NB, 2 * P).rearrange("p (a c) -> p a c", a=2)
        TIX = cut(P, SC).bitcast(I32)
        TAILI = cut(1, 3 * P).bitcast(I32)
        MTAIL = cut(P - TAIL, RW)
        NEXT, NEXTF, BAD = cut(EP - 1, 1).bitcast(I32), cut(EP - 1, 1), cut(P, 2)
        FLAG = sb("FLAG", [1, 1], I32)
        s_f, s_fv, s_fp, s_fx = sem("s_f"), sem("s_fv"), sem("s_fp"), [sem("s_fx0"), sem("s_fx1")]
        n_full = (ET - 1) * P

        def group_edges():
            gw = G[:].rearrange("p r k w -> p (r k w)")
            raw, rawf, cols = gw[:, 0:3 * P].bitcast(I32), gw[:, 3 * P:6 * P], gw[:, 6 * P:9 * P].rearrange("p (f t) -> p f t", f=3)
            sm = gw[:, 9 * P:9 * P + 32]
            fields, place, kbi = sm[:, 0:3].bitcast(I32), sm[:, 3:6].bitcast(I32), sm[:, 6:7].bitcast(I32)
            kb, pos, hi, out_, placef = sm[:, 7:8], sm[:, 8:9], sm[:, 9:10], sm[:, 10:11], sm[:, 11:14]
            posi = sm[:, 14:15].bitcast(I32)
            ko = OH[:, 0].rearrange("p k n -> p (k n)").bitcast(BF16)[:, 0:NB]
            junk = OH[:, 1].rearrange("p k n -> p (k n)")[:, 0:NB]
            rk = PS[7][:, 0:NB]
            flat = ET2.rearrange("t (e o) -> (t e) o", o=1)
            chunks = -(-ET // P)

            def out_of_order(q):
                return q.value_load(FLAG[0:1, 0:1], min_val=0, max_val=1)

            with nc.Block() as block:
                @block.sync
                def _(q):
                    with q.If(out_of_order(q) > 0):
                        for n in range(chunks):
                            k = min(P, ET - n * P)
                            q.wait_ge(s_fv, 3 * n if n else 1)
                            q.dma_start(raw[0:k, :], ET1[n * P:n * P + k, :]).then_inc(s_f, 16)
                        for half in range(2):
                            q.wait_ge(s_fx[half], 48 * (chunks * P // 2))
                        q.dma_start(ET1[0:ET - 1, :], ET2[0:ET - 1, :]).then_inc(s_f, 16)
                        for f in range(3):
                            q.dma_start(ET1[ET - 1:ET, f * P:f * P + TAIL], ET2[ET - 1:ET, f * P:f * P + TAIL]).then_inc(s_f, 16)
                        q.wait_ge(s_f, 16 * (chunks + 4))

                @block.vector
                def _(q):
                    with q.If(out_of_order(q) > 0):
                        c = Chain(q, s_fc)
                        c.step(q.memset(raw, -1))
                        for n in range(chunks):
                            if n == 0:
                                q.sem_inc(s_fv, 1)
                            q.wait_ge(s_f, 16 * (n + 1))
                            c.step(q.tensor_copy(rawf, raw))
                            c.step(q.memset(raw, -1))
                            q.sem_inc(s_fv, 3 if n else 2)
                            q.wait_ge(s_fp, 1 + n * (1 + 2 * P) + 1)
                            c.step(q.tensor_copy(cols, PS[6][:, 0:3 * P].rearrange("p (f t) -> p f t", f=3)))
                            with q.Fori(0, P) as t:
                                c.enter(t, 11)
                                dcol = cols[:, 0, bass.ds(t, 1)]
                                c.inc(q.tensor_scalar(out_, dcol, 0.0, None, ALU.is_lt))
                                c.step(q.tensor_copy(fields, cols[:, :, bass.ds(t, 1)].rearrange("p f t -> p (f t)")))
                                c.step(q.tensor_scalar(kbi, fields[:, 0:1], 7, None, ALU.arith_shift_right))
                                c.step(q.tensor_copy(kb, kbi))
                                q.wait_ge(s_fp, t * 2 + (1 + n * (1 + 2 * P) + 1))
                                c.step(q.tensor_scalar(ko, IOTA[:, 0:NB], kb, None, ALU.is_equal))
                                q.sem_inc(s_fk, 1)
                                q.wait_ge(s_fp, t * 2 + (1 + n * (1 + 2 * P) + 2))
                                c.step(q.tensor_tensor_reduce(out=junk, in0=rk, in1=ko, scale=1.0, scalar=0.0, op0=ALU.mult,
                                                              op1=ALU.add, accum_out=pos))
                                q.sem_inc(s_fk, 1)
                                c.step(q.scalar_tensor_tensor(pos, out_, FAR, pos, ALU.mult, ALU.add))
                                c.step(q.tensor_copy(posi, pos))
                                c.step(q.tensor_scalar(kbi, posi, 7, None, ALU.arith_shift_right))
                                c.step(q.tensor_copy(hi, kbi))
                                c.step(q.scalar_tensor_tensor(pos, hi, 2.0 * P, pos, ALU.mult, ALU.add))
                                q.sem_inc(s_fk, 1)
                                q.wait_ge(s_fd, t + (n * P + 1))
                                c.leave(P)

                @block.gpsimd
                def _(q):
                    with q.If(out_of_order(q) > 0):
                        with q.Fori(0, chunks * P // 2) as u:
                            for half in range(2):
                                t = 2 * u + half
                                q.wait_ge(s_fk, 3 * t + 3)
                                q.nop(nofuse=True)
                                for f in range(3):
                                    q.tensor_scalar(placef[:, f:f + 1], pos, float(f * P), None, ALU.add).then_inc(s_fg, 1)
                                q.wait_ge(s_fg, 6 * t + 3)
                                q.nop(nofuse=True)
                                for f in range(3):
                                    q.tensor_copy(place[:, f:f + 1], placef[:, f:f + 1]).then_inc(s_fg, 1)
                                q.wait_ge(s_fg, 6 * t + 6)
                                q.nop(nofuse=True)
                                for f in range(3):
                                    q.indirect_dma_start(flat, bass.IndirectOffsetOnAxis(ap=place[:, f:f + 1], axis=0), fields[:, f:f + 1],
                                                         None, bounds_check=ET * 3 * P - 1, oob_is_err=False).then_inc(s_fx[half], 16)
                                q.wait_ge(s_fx[half], 48 * u + 48)
                                q.sem_inc(s_fd, 1)

                @block.tensor
                def _(q):
                    with q.If(out_of_order(q) > 0):
                        q.matmul(rk, ONES[0:EP, :], CNTA[:, 0:NB], start=True, stop=False, skip_group_check=True).then_inc(s_fp, 1)
                        for n in range(chunks):
                            q.wait_ge(s_fv, 3 * n + 3)
                            for f in range(3):
                                m = q.transpose(PS[6][:, f * P:(f + 1) * P], rawf[:, f * P:(f + 1) * P], IDENT[:])
                            m.then_inc(s_fp, 1)
                            with q.Fori(0, P) as t:
                                q.wait_ge(s_fk, 3 * t + (3 * n * P + 1))
                                q.matmul(rk, USTB[:], ko, start=False, stop=False, skip_group_check=True).then_inc(s_fp, 1)
                                q.wait_ge(s_fk, 3 * t + (3 * n * P + 2))
                                q.matmul(rk, LINB[:], ko, start=False, stop=False, skip_group_check=True).then_inc(s_fp, 1)

        s_fk, s_fd, s_fg, s_fc = sem("s_fk"), sem("s_fd"), sem("s_fg"), sem("s_fc")
        with nc.Block() as block:
            @block.sync
            def _(q):
                q.dma_start(EDG[0][0:EP, :].bitcast(I32), dst.rearrange("(p c) -> p c", p=EP)).then_inc(s_ld[0], 16)
                q.dma_start(EDG[1][0:EP, :].bitcast(I32), src.rearrange("(p c) -> p c", p=EP)).then_inc(s_ld[1], 16)
                q.dma_start(X[:, 0:NB - 1, :], x[0:(NB - 1) * P, :].rearrange("(b p) d -> p b d", p=P)).then_inc(s_ld[2], 16)
                q.wait_ge(s_v, 1)
                q.dma_start(X[0:LAST, NB - 1, :], x[(NB - 1) * P:N, :]).then_inc(s_ld[2], 16)
                q.dma_start(NEXT[0:EP - 1, :], dst[EC:E].rearrange("(p c) -> p c", c=EC)[:, 0:1],
                            allow_slow_non_contiguous=True).then_inc(s_ld[5], 16)
                q.wait_ge(s_ld[2], 32)

            @block.scalar
            def _(q):
                for f, a in enumerate((dst, src, etype)):
                    q.dma_start(ET1[0:ET - 1, f * P:(f + 1) * P], a[0:n_full].rearrange("(t e) -> t e", e=P)).then_inc(s_ld[3], 16)
                    q.dma_start(ET1[ET - 1:ET, f * P:f * P + TAIL], a[n_full:E].rearrange("(t e) -> t e", t=1)).then_inc(s_ld[3], 16)
                q.wait_ge(s_v, 2)
                for f in range(3):
                    q.dma_start(ET1[ET - 1:ET, f * P + TAIL:(f + 1) * P], TAILI[0:1, f * P + TAIL:(f + 1) * P]).then_inc(s_ld[3], 16)
                q.dma_start(MSG[E:EROWS, :], MTAIL[:, :]).then_inc(s_ld[4], 16)
                q.wait_ge(s_cnt, 1)
                with q.Fori(0, (NB + 1) // len(SIGNS)) as j:
                    for u, signs in enumerate(SIGNS):
                        b = j * len(SIGNS) + u
                        if u == 0:
                            q.wait_ge(s_cnt, b + 1)
                        q.activation(signs[0:EP, :], SRCF[0:EP, :], ACT.Sign, bias=NTHR[0:EP, bass.ds(b, 1)],
                                     accum_out=CNTB[:, bass.ds(b, 1)]).then_inc(s_cnt, 1)
                q.wait_ge(s_ld[4], 16)

            @block.gpsimd
            def _(q):
                c = Chain(q, s_pk)
                c.step(q.iota(IOTI[:, 0:P], pattern=[[1, P]], base=0, channel_multiplier=0))
                c.step(q.tensor_copy(IOTA[:], IOTI[:, 0:P]))
                c.step(q.iota(IOTI[:, 0:NB + 1], pattern=[[P, NB + 1]], base=0, channel_multiplier=0))
                c.step(q.tensor_copy(THR, IOTI[:, 0:NB + 1]))
                c.step(q.iota(IOTI[:, 0:1], pattern=[[0, 1]], base=0, channel_multiplier=1))
                c.step(q.tensor_copy(PCOL[:], IOTI[:, 0:1]))
                c.step(q.iota(IOTI[:, 0:SC], pattern=[[P, SC]], base=0, channel_multiplier=1))
                c.step(q.tensor_copy(ISTEP, IOTI[:, 0:SC]))
                c.step(q.iota(IOTI[:, 0:SW], pattern=[[1, SW]], base=0, channel_multiplier=0))
                c.step(q.tensor_copy(ITER, IOTI[:, 0:SW]))
                q.wait_ge(s_ld[3], 9 * 16)
            @block.vector
            def _(q):
                q.memset(X[:, NB - 1, :], 0.0).then_inc(s_v, 1)
                c = Chain(q, s_k)
                chains.append(c)
                c.inc(q.memset(MTAIL, 0.0))
                c.inc(q.memset(TAILI, 0))
                c.inc(q.memset(ONES[:], 1.0))
                c.hold()
                c.inc(q.memset(MTAIL[:, D + 1:D + 2], -FAR))
                c.inc(q.memset(TAILI[:, 0:P], -1))
                c.hold()
                q.sem_inc(s_v, 1)
                q.wait_ge(s_pk, 10)
                c.inc(q.tensor_scalar(IDENT[:], IOTA[:], PCOL[:], None, ALU.is_equal))
                c.inc(q.tensor_scalar(UST[:], IOTA[:], PCOL[:], None, ALU.is_gt))
                c.inc(q.tensor_scalar(USTB[:], IOTA[:], PCOL[:], None, ALU.is_gt))
                c.inc(q.tensor_scalar(LINB[:], IOTA[:], PCOL[:], None, ALU.is_le))
                c.inc(q.memset(BAD, 0.0))
                c.inc(q.tensor_scalar(NTHR, THR, -1.0, 0.5, ALU.mult, ALU.add))
                q.wait_ge(s_ld[1], 16)
                c.inc(q.tensor_copy(SRCF[0:EP, :], EDG[1][0:EP, :].bitcast(I32)))
                c.hold()
                q.sem_inc(s_cnt, 1)
                q.wait_ge(s_ld[0], 16)
                c.step(q.tensor_copy(EDF[0:EP, :], EDG[0][0:EP, :].bitcast(I32)))
                with q.Fori(0, (NB + 1) // len(JUNKS)) as j:
                    c.enter(j, len(JUNKS))
                    for u, junk in enumerate(JUNKS):
                        b = j * len(JUNKS) + u
                        q.wait_ge(s_k, c.at + c.n - len(JUNKS) + 1)
                        c.inc(q.tensor_scalar(junk[0:EP, :], EDF[0:EP, :], THR[0:EP, bass.ds(b, 1)], 0.0,
                                              ALU.is_lt, ALU.add, accum_out=CNTA[:, bass.ds(b, 1)]))
                    c.leave((NB + 1) // len(JUNKS))
                c.hold()
                q.wait_ge(s_cnt, 1 + NB + 1)
                c.step(q.tensor_scalar(CNTB[:], CNTB[:], -0.5, EC / 2.0, ALU.mult, ALU.add))
                q.wait_ge(s_ld[5], 16)
                c.step(q.tensor_copy(NEXTF, NEXT))
                c.inc(q.tensor_tensor(JUNK[0:EP, 0:EC - 1], EDF[0:EP, 1:EC], EDF[0:EP, 0:EC - 1], ALU.is_lt))
                c.inc(q.tensor_tensor(BAD[0:EP - 1, 1:2], NEXTF[0:EP - 1, :], EDF[0:EP - 1, EC - 1:EC], ALU.is_lt))
                c.hold()
                c.step(q.tensor_reduce(BAD[0:EP, 0:1], JUNK[0:EP, 0:EC - 1], AX.X, ALU.add))
                c.step(q.tensor_tensor(BAD[0:EP, 0:1], BAD[0:EP, 0:1], BAD[0:EP, 1:2], ALU.add))
                q.sem_inc(s_bad, 1)
                q.wait_ge(s_bad, 2)
                c.step(q.tensor_scalar(BAD[:, 1:2], PS[7][:, 0:1], 0.0, None, ALU.is_gt))
                c.step(q.tensor_copy(FLAG[:], BAD[0:1, 1:2]))

            @block.tensor
            def _(q):
                q.wait_ge(s_bad, 1)
                q.matmul(PS[7][:, 0:1], ONES[0:EP, :], BAD[0:EP, 0:1], start=True, stop=True).then_inc(s_bad, 1)

        group_edges()

        with nc.Block() as block:
            @block.gpsimd
            def _(q):
                q.wait_ge(s_tix, 1)
                for col in range(SC):
                    if col >= 2:
                        q.wait_ge(s_tix, col)
                    q.indirect_dma_start(EGI[col % 2], None, ET1,
                                         bass.IndirectOffsetOnAxis(ap=TIX[:, col:col + 1], axis=0)).then_inc(s_eg, 16)
                    q.wait_ge(s_eg, 16 * (col + 1))

            @block.vector
            def _(q):
                c = chains[0]
                pe = 0
                for s, (breg, treg) in enumerate(((BREGA, None), (BREGB, TREGB))):
                    q.sem_inc(s_v, 1)
                    pe += 1
                    q.wait_ge(s_pe, pe)
                    c.step(q.tensor_copy(SE, PS[0][0:NB, 0:2]))
                    start, end = SE[:, 0:1], SE[:, 1:2]
                    c.inc(q.tensor_copy(FL[:, 0:1], start))
                    c.inc(q.tensor_scalar(COL[:, 0:1], end, -1.0, None, ALU.add))
                    c.inc(q.tensor_tensor(COL[:, 1:2], end, start, ALU.is_gt))
                    c.hold()
                    c.step(q.tensor_copy(FL[:, 1:2], COL[:, 0:1]))
                    c.step(q.tensor_scalar(FL, FL, 7, None, ALU.arith_shift_right))
                    c.step(q.tensor_copy(COL[:, 2:4], FL))
                    c.step(q.tensor_tensor(COL[:, 4:5], COL[:, 3:4], COL[:, 2:3], ALU.subtract))
                    c.step(q.scalar_tensor_tensor(COL[:, 5:6], COL[:, 4:5], 1.0, COL[:, 1:2], ALU.add, ALU.mult))
                    q.sem_inc(s_v, 1)
                    pe += 1
                    q.wait_ge(s_pe, pe)
                    c.step(q.tensor_copy(COL[:, 6:7], PS[1][0:NB, 0:1]))
                    c.inc(q.tensor_tensor(COL[:, 7:8], COL[:, 6:7], COL[:, 5:6], ALU.add))
                    c.inc(q.tensor_tensor(RH[:, 1:2], COL[:, 2:3], COL[:, 6:7], ALU.subtract))
                    c.inc(q.tensor_scalar(RH[:, 0:1], PCOL[0:NB, :], float(-NB), None, ALU.add))
                    c.hold()
                    c.inc(q.tensor_scalar(BW[:, 0, :], ONES[0:NB, :], RH[:, 0:1], None, ALU.mult))
                    c.inc(q.tensor_scalar(BW[:, 1, :], ONES[0:NB, :], RH[:, 1:2], None, ALU.mult))
                    c.inc(q.tensor_scalar(TMPW[0:NB, :], ITER[0:NB, :], COL[:, 7:8], None, ALU.is_ge))
                    c.inc(q.tensor_scalar(SELX[0:NB, :], ITER[0:NB, :], COL[:, 6:7], None, ALU.is_ge))
                    c.hold()
                    c.step(q.tensor_tensor(SELX[0:NB, :], SELX[0:NB, :], TMPW[0:NB, :], ALU.subtract))
                    q.sem_inc(s_v, 1)
                    pe += 1
                    q.wait_ge(s_pe, pe)
                    bstep = SLOB[:] if s else DSTA[:]
                    for k in range(0, SW, 512):
                        w = min(512, SW - k)
                        c.inc(q.tensor_scalar(bstep[:, k:k + w], PS[2 + k // 512][:, 0:w], float(NB), None, ALU.add))
                    c.hold()
                    c.step(q.tensor_scalar(TMPW[0:1, :], bstep[0:1, :], float(NB - 1), None, ALU.min))
                    c.inc(q.tensor_copy(breg[:], TMPW[0:1, :]))
                    c.inc(q.tensor_scalar(bstep, bstep, float(P), None, ALU.mult))
                    c.hold()
                    q.sem_inc(s_v, 1)
                    pe += 1
                    q.wait_ge(s_pe, pe)
                    if s:
                        for k in range(0, SW, 512):
                            w = min(512, SW - k)
                            c.inc(q.tensor_tensor(TMPW[0:1, k:k + w], PS[2 + k // 512][0:1, 0:w], ITER[0:1, k:k + w], ALU.add))
                        c.hold()
                        c.step(q.tensor_scalar(TMPW[0:1, :], TMPW[0:1, :], float(ET - 1), None, ALU.min))
                        c.step(q.tensor_copy(treg[:], TMPW[0:1, :]))
                        continue
                    tl = PS[2][:, 0:SC]
                    c.step(q.tensor_tensor(TMPW[:, 0:SC], tl, ISTEP, ALU.add))
                    c.step(q.tensor_scalar(TMPW[:, 0:SC], TMPW[:, 0:SC], float(ET - 1), None, ALU.min))
                    c.step(q.tensor_copy(TIX, TMPW[:, 0:SC]))
                    q.sem_inc(s_tix, 1)
                    for col in range(SC):
                        q.wait_ge(s_eg, 16 * (col + 1))
                        c.step(q.tensor_copy(EGF, EGI[col % 2]))
                        q.sem_inc(s_tix, 1)
                        pe += 1
                        q.wait_ge(s_pe, pe)
                        at = slice(col * P, (col + 1) * P)
                        c.inc(q.tensor_tensor(DLOA[:, at], PS[6][:, 0:P], DSTA[:, at], ALU.subtract))
                        c.hold()
                        c.inc(q.tensor_copy(DSTA[:, at], PS[6][:, 0:P]))
                        c.inc(q.tensor_scalar(POSA[:, at], PS[6][:, P:2 * P], float(R), None, ALU.mult))
                        c.hold()
                        c.step(q.tensor_tensor(POSA[:, at], POSA[:, at], PS[6][:, 2 * P:3 * P], ALU.add))
                        c.step(q.tensor_copy(IDXA[:, at], POSA[:, at]))
                        q.sem_inc(s_v, 1)

            @block.tensor
            def _(q):
                v = 2
                for s, cnt in ((0, CNTA), (1, CNTB)):
                    v += 1
                    q.wait_ge(s_v, v)
                    q.matmul(PS[0][0:NB, 0:1], cnt[:, 0:NB], ONES[0:EP, 0:1], start=True, stop=True)
                    q.matmul(PS[0][0:NB, 1:2], cnt[:, 1:NB + 1], ONES[0:EP, 0:1], start=True, stop=True).then_inc(s_pe, 1)
                    v += 1
                    q.wait_ge(s_v, v)
                    q.matmul(PS[1][0:NB, 0:1], UST[0:NB, 0:NB], COL[:, 5:6], start=True, stop=True).then_inc(s_pe, 1)
                    v += 1
                    q.wait_ge(s_v, v)
                    for k in range(0, SW, 512):
                        w = min(512, SW - k)
                        last = q.matmul(PS[2 + k // 512][:, 0:w], BW[:, 0, :], SELX[0:NB, k:k + w], start=True, stop=True)
                    last.then_inc(s_pe, 1)
                    v += 1
                    q.wait_ge(s_v, v)
                    if s:
                        for k in range(0, SW, 512):
                            w = min(512, SW - k)
                            last = q.matmul(PS[2 + k // 512][:, 0:w], BW[:, 1, :], SELX[0:NB, k:k + w], start=True, stop=True)
                        last.then_inc(s_pe, 1)
                        continue
                    for col in range(SC):
                        last = q.matmul(PS[2][:, col:col + 1], SELX[0:NB, col * P:(col + 1) * P], RH[:, 1:2], start=True, stop=True)
                    last.then_inc(s_pe, 1)
                    for col in range(SC):
                        q.wait_ge(s_tix, col + 2)
                        for f in range(3):
                            last = q.transpose(PS[6][:, f * P:(f + 1) * P], EGF[:, f * P:(f + 1) * P], IDENT[:])
                        last.then_inc(s_pe, 1)
                        v += 1
                        q.wait_ge(s_v, v)
        spare = {}
        XW = X[:].rearrange("p b d -> p (b d)")
        AD = ACC[:, :, 0:D]
        GW = G[:].rearrange("p r k w -> p (r k w)")
        HROWV = HROW.rearrange("(b p) w -> p b w", p=P)
        SIW, MJW = SI[:].rearrange("p b h -> p (b h)"), MJ[:].rearrange("p b h -> p (b h)")

        def wait(q, s, v):
            if not (isinstance(v, int) and v <= 0):
                q.wait_ge(s, v)

        def is_first(g):
            return isinstance(g, int) and g == 0

        def loop(q, times, body):
            body(0)
            with q.Fori(1, times) as j:
                body(j)

        def acc_of(reg, w):
            return words[:, bass.ds(reg * RW, w)]

        def words_of(q, table, at, n, top):
            if q.engine not in spare:
                spare[q.engine] = [q.alloc_register(f"word{k}") for k in range(K)]
            regs = spare[q.engine][:n]
            q.load(regs, table[0:1, bass.ds(at, n)])
            return [q.snap(r, min_val=0, max_val=top) for r in regs]

        def blocks(q, breg, g):
            return words_of(q, breg, g * K, K, NB - 1)

        pool = [sem(f"work{i}") for i in range(20)]
        assert [s.num for s in pool] == list(range(pool[0].num, pool[0].num + len(pool)))
        in_use = [0]

        def own(name):
            in_use[0] += 1
            return pool[in_use[0] - 1]

        def fresh():
            if in_use[0]:
                with nc.Block() as block:
                    @block.sync
                    def _(q):
                        q.sem_clear(range(pool[0].num, pool[0].num + in_use[0]))
            in_use[0] = 0

        def norm_vector(q, c, s_var, s_std, s_norm):
            with q.Fori(0, NB // 2) as j:
                c.enter(j, 2)
                for u in range(2):
                    b = j * 2 + u
                    c.inc(q.bn_stats(ST6[:].rearrange("p b s -> p (b s)")[:, bass.ds(b * 6, 6)], XW[:, bass.ds(b * D, D)]))
                c.leave(NB // 2)
            c.hold()
            even, odd = ST6[:, :, 1], ST6[:, :, 4]
            c.inc(q.tensor_tensor(MV[:, :, 0], even, odd, ALU.add))
            c.inc(q.tensor_tensor(NMR[:], even, odd, ALU.subtract))
            c.inc(q.tensor_tensor(MV[:, :, 1], ST6[:, :, 2], ST6[:, :, 5], ALU.add))
            c.hold()
            c.inc(q.tensor_scalar(MV[:, :, 0], MV[:, :, 0], 0.5, None, ALU.mult))
            c.step(q.scalar_tensor_tensor(NMR[:], NMR[:], 0.25, NMR[:], ALU.mult, ALU.mult))
            c.step(q.scalar_tensor_tensor(MV[:, :, 1], MV[:, :, 1], 1.0 / D, NMR[:], ALU.mult, ALU.add))
            c.step(q.tensor_scalar(RSTD[:], MV[:, :, 1], LN_EPS, None, ALU.add))
            q.sem_inc(s_var, 1)
            q.wait_ge(s_std, 1)
            c.step(q.reciprocal(RSTD[:], RSTD[:]))
            c.step(q.scalar_tensor_tensor(NMR[:], MV[:, :, 0], -1.0, RSTD[:], ALU.mult, ALU.mult))
            q.sem_inc(s_norm, 1)

        def norm_scalar(q, s_var, s_std, s_norm):
            q.wait_ge(s_var, 1)
            q.activation(RSTD[:], RSTD[:], ACT.Sqrt).then_inc(s_std, 1)
            q.wait_ge(s_norm, 1)

        def overlapped(q, front, back):
            def body(j):
                for u in range(2):
                    front(u, j * 2 + u)
                    if u or not is_first(j):
                        back(1 - u, j * 2 + u - 1, j - 1 + u)
            body(0)
            body(1)
            with q.Fori(2, NB // 2) as j:
                body(j)
            back(1, NB - 1, NB // 2 - 1)

        def dense(tag, normed, load, width, bias_at, table, before=None, prepare=None):
            fresh()
            s_w, s_var, s_std, s_norm, s_ch = own(tag + "w"), own(tag + "var"), own(tag + "std"), own(tag + "norm"), own(tag + "ch")
            s_h, s_tr, s_ht, s_mm, s_ea, s_ev = (own(tag + n) for n in ("h", "tr", "ht", "mm", "ea", "ev"))
            s_st = [own(tag + f"st{u}") for u in range(2)] if table else []
            s_o = own(tag + "o")
            tw = bias_at // 2
            stage = SCR[:].rearrange("p (u a) c -> p u (a c)", u=2)
            tabv = TAB.rearrange("(b p r) d -> p b (r d)", p=P, r=R)
            aw = width - bias_at
            evs = 2 if table or aw > RW else 1
            with nc.Block() as block:
                @block.sync
                def _(q):
                    n = load(q, s_w)
                    if table:
                        def body(j):
                            for u in range(2):
                                b = j * 2 + u
                                q.wait_ge(s_ea, b + 1)
                                q.wait_ge(s_ev, b * 2 + 1)
                                q.dma_start(tabv[:, bass.ds(b, 1), :], stage[:, u:u + 1, :]).then_inc(s_st[u], 16)
                        with q.Fori(0, NB // 2) as j:
                            body(j)
                        for s in s_st:
                            q.wait_ge(s, 16 * (NB // 2))
                    else:
                        q.wait_ge(s_ev, NB * evs)
                        q.dma_start(HROWV, ACC[:]).then_inc(s_o, 16)
                        q.wait_ge(s_o, 16)

                @block.scalar
                def _(q):
                    if normed:
                        norm_scalar(q, s_var, s_std, s_norm)

                    def front(u, b):
                        wait(q, s_tr, b - 1)
                        if normed:
                            q.activation(HB[:, u, :], XW[:, bass.ds(b * D, D)], ACT.Relu,
                                         bias=NMR[:, bass.ds(b, 1)], scale=RSTD[:, bass.ds(b, 1)]).then_inc(s_h, 1)
                        else:
                            q.activation(HB[:, u, :], words[:, bass.ds(b * RW, D)], ACT.Relu).then_inc(s_h, 1)

                    def back(u, b, j):
                        if table:
                            q.wait_ge(s_mm, b + 1)
                            wait(q, s_st[u], j * 16)
                            q.copy(stage[:, u, 0:tw], PS[2 + 3 * u][:, 0:tw]).then_inc(s_ea, 1)
                    overlapped(q, front, back)

                @block.vector
                def _(q):
                    c = Chain(q, s_ch)
                    if before:
                        before(q, c)
                    if normed:
                        norm_vector(q, c, s_var, s_std, s_norm)
                    if prepare:
                        prepare(q, c, s_w)
                        q.sem_inc(s_norm, 1)

                    def front(u, b):
                        q.wait_ge(s_tr, b + 1)
                        wait(q, s_mm, b - 1)
                        q.tensor_copy(HT[:, u, :], PS[u][:, 0:D]).then_inc(s_ht, 1)

                    def back(u, b, j):
                        q.wait_ge(s_mm, b + 1)
                        if table:
                            wait(q, s_st[u], j * 16)
                            q.tensor_copy(stage[:, u, tw:2 * tw], PS[3 + 3 * u][:, 0:tw]).then_inc(s_ev, 1)
                        if aw > RW:
                            q.tensor_tensor(SIW[:, bass.ds(b * 2 * HEADS, HEADS)], PS[4 + 3 * u][:, RW:aw], BIAS[:, RW:aw],
                                            ALU.add).then_inc(s_ev, 1)
                        q.tensor_tensor(words[:, bass.ds(b * RW, min(aw, RW))], PS[4 + 3 * u][:, 0:min(aw, RW)],
                                        BIAS[:, 0:min(aw, RW)], ALU.add).then_inc(s_ev, 1)
                    overlapped(q, front, back)

                @block.tensor
                def _(q):
                    if prepare:
                        q.wait_ge(s_norm, 2)
                    else:
                        q.wait_ge(s_w, load.total)

                    def front(u, b):
                        q.wait_ge(s_h, b + 1)
                        wait(q, s_ht, b - 1)
                        q.transpose(PS[u][:, 0:D], HB[:, u, :], IDENT[:]).then_inc(s_tr, 1)

                    def back(u, b, j):
                        q.wait_ge(s_ht, b + 1)
                        wait(q, s_ev, (b - 1) * evs)
                        if table:
                            wait(q, s_ea, b - 1)
                            q.matmul(PS[2 + 3 * u][:, 0:tw], HT[:, u, :], WT[:, 0:tw], start=True, stop=True)
                            q.matmul(PS[3 + 3 * u][:, 0:tw], HT[:, u, :], WT[:, tw:2 * tw], start=True, stop=True)
                        q.matmul(PS[4 + 3 * u][:, 0:aw], HT[:, u, :], WT[:, bias_at:width], start=True, stop=True).then_inc(s_mm, 1)
                    overlapped(q, front, back)

        def load_relations(W, wl, bias):
            def load(q, s):
                q.dma_start(WT[:, 0:R * D].rearrange("d (r h) -> d r h", r=R), W.rearrange("r d h -> d r h")).then_inc(s, 16)
                q.dma_start(WT[:, R * D:(R + 1) * D], wl).then_inc(s, 16)
                q.dma_start(BIAS[:, 0:D], bias.partition_broadcast(P)).then_inc(s, 16)
            load.total = 48
            return load

        def one_hot(q, r, dlo, g, op=ALU.is_equal):
            return q.tensor_tensor(OH[:, r % 2], bcast(IOTA[:].unsqueeze(1), P, K, P),
                                   bcast(dlo[:, bass.ds(g * K, K)].unsqueeze(2), P, K, P), op)

        def slot(k):
            return PS[k // 2][:, (k % 2) * 256:(k % 2) * 256 + RW]

        def groups(q, body):
            def ring(j):
                for r in range(RING):
                    body(j, r, j * RING + r)
            loop(q, NG // RING, ring)

        def add_half(q, s_mm, s_add, regs, g, h, w):
            wait(q, s_mm, 2 * g + h + 1)
            for k in range(K // 2):
                wait(q, s_add, g * K + h * K // 2 + k)
                a = acc_of(regs[k], w)
                q.tensor_tensor(a, a, slot(h * 4 + k)[:, 0:w], ALU.add).then_inc(s_add, 1)

        def gather(q, r, table, row, s_got):
            for k in range(K):
                q.indirect_dma_start(G[:, r, k, 0:row], None, table,
                                     bass.IndirectOffsetOnAxis(ap=IDS[:, r, k:k + 1], axis=0)).then_inc(s_got[r], 16)

        def sum_pass(tag, table, row, w, rank):
            fresh()
            s_ids, s_oh, s_mm, s_add = own(tag + "ids"), own(tag + "oh"), own(tag + "mm"), own(tag + "add")
            s_got = [sem(tag + f"got{r}") for r in range(RING)]
            s_cs, s_key, s_rk, s_pos, s_rc = (own(tag + n) for n in ("cs", "key", "rk", "pos", "rc")) if rank else [None] * 5
            KO = SCR[:].rearrange("p a c -> p (a c)").bitcast(BF16)[:, 0:2 * K * NB].rearrange("p (u k b) -> p u k b", u=2, k=K)
            RK = PS[4][:, 0:NB]
            with nc.Block() as block:
                @block.scalar
                def _(q):
                    def body(j, r, g):
                        wait(q, s_mm, 2 * (g - RING + 1))
                        q.copy(IDS[:, r, :], IDXA[:, bass.ds(g * K, K)]).then_inc(s_ids, 1)
                    groups(q, body)

                @block.gpsimd
                def _(q):
                    def body(j, r, g):
                        wait(q, s_ids, g + 1)
                        q.nop(nofuse=True)
                        gather(q, r, table, row, s_got)
                    groups(q, body)

                @block.vector
                def _(q):
                    if rank:
                        c = Chain(q, s_cs)

                    def keys(j, r, g):
                        at = bass.ds(g * K, K)
                        kbi = SM[:, 0, 0:K].bitcast(I32)
                        kb, below, inv = SM[:, 1, 0:K], SM[:, 2, 0:K], SM[:, 3 + r % 2, 0:K]
                        c.inc(q.tensor_scalar(kbi, IDXA[:, at], 10, None, ALU.arith_shift_right))
                        c.inc(q.tensor_scalar(below, DLOA[:, at], 0.0, None, ALU.is_lt))
                        c.hold()
                        c.inc(q.tensor_copy(kb, kbi))
                        c.inc(q.scalar_tensor_tensor(inv, DLOA[:, at], float(P - 1), below, ALU.is_gt, ALU.add))
                        c.hold()
                        c.step(q.scalar_tensor_tensor(kb, inv, 200.0, kb, ALU.mult, ALU.add))
                        q.tensor_tensor(KO[:, r % 2], bcast(IOTA[:, 0:NB].unsqueeze(1), P, K, NB),
                                        bcast(kb.unsqueeze(2), P, K, NB), ALU.is_equal).then_inc(s_key, 1)

                    def ranks(j, r, g, h, regs):
                        first = g * K + (h - 1) * K // 2
                        if regs:
                            wait(q, s_mm, 2 * g + h)
                        for k in range(K // 2):
                            kk = h * 4 + k
                            if regs:
                                wait(q, s_add, first + k)
                                a = acc_of(regs[k], w)
                                q.tensor_tensor(a, a, slot((1 - h) * 4 + k)[:, 0:w], ALU.add).then_inc(s_add, 1)
                            q.wait_ge(s_rk, 2 * (g * K + kk) + 2)
                            q.tensor_tensor_reduce(out=HT[:, 0, 0:NB], in0=RK, in1=KO[:, r % 2, kk, :], scale=1.0, scalar=0.0,
                                                   op0=ALU.mult, op1=ALU.add, accum_out=SM[:, 5, kk:kk + 1]).then_inc(s_pos, 1)

                    def body(j, r, g):
                        wait(q, s_mm, 2 * (g - 1))
                        one_hot(q, r, DLOA, g).then_inc(s_oh, 1)
                        if not rank:
                            regs = blocks(q, BREGA, g)
                            for h in range(2):
                                add_half(q, s_mm, s_add, regs[h * 4:h * 4 + 4], g, h, w)
                            return
                        keys(j, r, g)
                        if is_first(g):
                            regs = words_of(q, BREGA, 0, K // 2, NB - 1)
                            ranks(j, r, g, 0, None)
                            ranks(j, r, g, 1, regs)
                        else:
                            regs = words_of(q, BREGA, g * K - K // 2, K, NB - 1)
                            ranks(j, r, g, 0, regs[0:4])
                            ranks(j, r, g, 1, regs[4:8])
                        q.wait_ge(s_pos, g * K + K)
                        c.step(q.scalar_tensor_tensor(POSA[:, bass.ds(g * K, K)], SM[:, 3 + r % 2, 0:K], FAR, SM[:, 5, 0:K],
                                                      ALU.mult, ALU.add))

                    def ring(j):
                        for r in range(RING):
                            body(j, r, j * RING + r)
                    ring(0)
                    per = c.n if rank else 0
                    with q.Fori(1, NG // RING) as j:
                        if rank:
                            c.at, c.n = per * j, 0
                        ring(j)
                    if rank:
                        add_half(q, s_mm, s_add, words_of(q, BREGA, NS - K // 2, K // 2, NB - 1), NG - 1, 1, w)

                @block.tensor
                def _(q):
                    if rank:
                        q.matmul(RK, ONES[0:EP, :], CNTB[:, 0:NB], start=True, stop=False, skip_group_check=True).then_inc(s_rk, 1)

                    def body(j, r, g):
                        q.wait_ge(s_got[r], 16 * K * (j + 1))
                        q.wait_ge(s_oh, g + 1)
                        if rank:
                            q.wait_ge(s_key, g + 1)
                        for h in range(2):
                            wait(q, s_add, (g - 1) * K + (h + 1) * K // 2)
                            for k in range(4):
                                kk = h * 4 + k
                                i = g * K + kk
                                if rank:
                                    q.matmul(RK, USTB[:], KO[:, r % 2, kk, :], start=False, stop=False, skip_group_check=True).then_inc(s_rk, 1)
                                m = q.matmul(slot(kk)[:, 0:w], OH[:, r % 2, kk, :], G[:, r, kk, 0:w], start=True, stop=True)
                                if k == 3:
                                    m.then_inc(s_mm, 1)
                                if rank:
                                    q.wait_ge(s_pos, i + 1)
                                    q.matmul(RK, LINB[:], KO[:, r % 2, kk, :], start=False, stop=False, skip_group_check=True).then_inc(s_rk, 1)
                    groups(q, body)
        def scatter_pass(tag):
            fresh()
            s_ids, s_oh, s_x, s_tr, s_ot, s_mm, s_cp, s_c = (own(tag + n) for n in ("ids", "oh", "x", "tr", "ot", "mm", "cp", "c"))
            s_sc = [sem(tag + f"sc{r}") for r in range(RING)]
            with nc.Block() as block:
                @block.scalar
                def _(q):
                    def body(j, r, g):
                        wait(q, s_sc[r], 16 * K * j)
                        q.copy(IDS[:, r, :], POSA[:, bass.ds(g * K, K)]).then_inc(s_ids, 1)
                        for h in range(2):
                            q.wait_ge(s_tr, 2 * g + h + 1)
                            wait(q, s_mm, 2 * g + h - 1)
                            q.copy(SCR[:, h, :], PS[4 + h][:]).then_inc(s_ot, 1)
                    groups(q, body)

                @block.vector
                def _(q):
                    c = Chain(q, s_c)
                    c.step(q.memset(GW, 0.0))
                    c.step(q.memset(G[:, :, :, D:D + 1], 1.0))

                    def body(j, r, g):
                        wait(q, s_tr, 2 * (g - 1))
                        one_hot(q, r, DLOA, g).then_inc(s_oh, 1)
                        wait(q, s_sc[r], 16 * K * j)
                        srci = SM[:, r, 0:K].bitcast(I32)
                        q.tensor_scalar(srci, IDXA[:, bass.ds(g * K, K)], 3, None, ALU.arith_shift_right).then_inc(s_x, 1)
                        q.tensor_copy(G[:, r, :, D + 2], DSTA[:, bass.ds(g * K, K)]).then_inc(s_x, 1)
                        q.wait_ge(s_x, 3 * g + 2)
                        q.tensor_copy(G[:, r, :, D + 1], srci).then_inc(s_x, 1)
                        for h in range(2):
                            q.wait_ge(s_mm, 2 * g + h + 1)
                            for n in range(2):
                                q.tensor_copy(G[:, r, h * 4 + 2 * n:h * 4 + 2 * n + 2, 0:D],
                                              PS[2 * h + n][:].rearrange("p (s w) -> p s w", s=2)[:, :, 0:D]).then_inc(s_cp, 1)
                    groups(q, body)

                @block.tensor
                def _(q):
                    def body(j, r, g):
                        regs = blocks(q, BREGA, g)
                        q.wait_ge(s_oh, g + 1)
                        for h in range(2):
                            wait(q, s_ot, 2 * g + h - 1)
                            for k in range(4):
                                m = q.transpose(PS[4 + h][:, k * P:(k + 1) * P], OH[:, r % 2, h * 4 + k, :], IDENT[:])
                            m.then_inc(s_tr, 1)
                        for h in range(2):
                            q.wait_ge(s_ot, 2 * g + h + 1)
                            wait(q, s_cp, 4 * (g - 1) + 2 * h + 2)
                            for k in range(4):
                                m = q.matmul(slot(h * 4 + k)[:, 0:D], SCR[:, h, k * P:(k + 1) * P], acc_of(regs[h * 4 + k], D),
                                             start=True, stop=True)
                            m.then_inc(s_mm, 1)
                    groups(q, body)

                @block.gpsimd
                def _(q):
                    def body(j, r, g):
                        q.wait_ge(s_ids, g + 1)
                        q.wait_ge(s_x, 3 * g + 3)
                        q.wait_ge(s_cp, 4 * g + 4)
                        q.nop(nofuse=True)
                        for k in range(K):
                            q.indirect_dma_start(MSG, bass.IndirectOffsetOnAxis(ap=IDS[:, r, k:k + 1], axis=0), G[:, r, k, :], None,
                                                 bounds_check=E - 1, oob_is_err=False).then_inc(s_sc[r], 16)
                    groups(q, body)
                    for s in s_sc:
                        q.wait_ge(s, 16 * K * (NG // RING))

        def message_pass(tag, w):
            fresh()
            s_oh, s_mm, s_add, s_c, s_z = (own(tag + n) for n in ("oh", "mm", "add", "c", "z"))
            s_got = [own(tag + f"got{r}") for r in range(RING)]
            tiles = MSG.rearrange("(t p) w -> t p w", p=P)
            with nc.Block() as block:
                def load(q, parity):
                    def body(j, r, g):
                        if r % 2 != parity:
                            return
                        regs = words_of(q, TREGB, g * K, K, ET - 1)
                        wait(q, s_mm, 2 * (g - RING + 1))
                        wait(q, s_oh, g - RING + 1)
                        for k in range(K):
                            q.dma_start(G[:, r, k, :], tiles[bass.ds(regs[k], 1), :, :].rearrange("o p w -> p (o w)")).then_inc(s_got[r], 16)
                    groups(q, body)

                @block.sync
                def _(q):
                    load(q, 0)

                @block.scalar
                def _(q):
                    load(q, 1)

                @block.gpsimd
                def _(q):
                    def body(j, r, g):
                        q.wait_ge(s_got[r], 16 * K * (j + 1))
                        q.nop(nofuse=True)
                        at = bass.ds(g * K, K)
                        q.tensor_copy(IDXB[:, at], G[:, r, :, D + 2]).then_inc(s_c, 1)
                        q.tensor_tensor(SLOB[:, at], G[:, r, :, D + 1], SLOB[:, at], ALU.subtract).then_inc(s_c, 1)
                    groups(q, body)

                @block.vector
                def _(q):
                    q.memset(words, 0.0).then_inc(s_z, 1)
                    q.wait_ge(s_z, 1)

                    def adds(g):
                        regs = blocks(q, BREGB, g)
                        for h in range(2):
                            add_half(q, s_mm, s_add, regs[h * 4:h * 4 + 4], g, h, w)

                    def body(j, r, g):
                        q.wait_ge(s_c, 2 * g + 2)
                        wait(q, s_mm, 2 * (g - 1))
                        one_hot(q, r, SLOB, g).then_inc(s_oh, 1)
                        if not is_first(g):
                            adds(g - 1)
                    groups(q, body)
                    adds(NG - 1)

                @block.tensor
                def _(q):
                    sums(q, s_got, s_oh, s_add, s_mm, w)

        def sums(q, s_got, s_oh, s_add, s_mm, w):
            def body(j, r, g):
                q.wait_ge(s_got[r], 16 * K * (j + 1))
                q.wait_ge(s_oh, g + 1)
                for h in range(2):
                    wait(q, s_add, (g - 1) * K + (h + 1) * K // 2)
                    for k in range(h * 4, h * 4 + 4):
                        m = q.matmul(slot(k)[:, 0:w], OH[:, r % 2, k, :], G[:, r, k, 0:w], start=True, stop=True)
                    m.then_inc(s_mm, 1)
            groups(q, body)

        STG = [GW[:, i * CH * D:(i + 1) * CH * D].rearrange("p (b d) -> p b d", b=CH) for i in range(2)]

        def load_rows(q, s_row, s_use):
            for n in range(NCH):
                wait(q, s_use, n - 1)
                q.dma_start(STG[n % 2], HROWV[:, n * CH:(n + 1) * CH, 0:D]).then_inc(s_row[n % 2], 16)

        def batch_norm_stage(tag):
            fresh()
            s_row, s_use, s_p, s_c, s_m, s_sq, s_pe, s_g = ([own(tag + "row0"), own(tag + "row1")], own(tag + "use"), own(tag + "p"),
                                                            own(tag + "c"), own(tag + "m"), own(tag + "sq"), own(tag + "pe"), own(tag + "g"))
            MEAN, VAR, GAM, BET = HB[:, 0, :], HB[:, 1, :], HT[:, 0, :], HT[:, 1, :]

            def node_sums(q, rows, blocks_of, first, last):
                b = 0
                while b < len(blocks_of):
                    n = min(4, len(blocks_of) - b)
                    if blocks_of[b + n - 1] == NB - 1 and n > 1:
                        n -= 1
                    k = LAST if blocks_of[b] == NB - 1 else P
                    m = q.matmul(PS[0][:, 0:n * D], ONES[0:k, :], rows[0:k, b:b + n, :], start=first and b == 0,
                                 stop=last and b + n == len(blocks_of), skip_group_check=True)
                    b += n
                return m

            with nc.Block() as block:
                @block.sync
                def _(q):
                    q.dma_start(GAM, gamma.partition_broadcast(P)).then_inc(s_g, 16)
                    q.dma_start(BET, beta.partition_broadcast(P)).then_inc(s_g, 16)
                    load_rows(q, s_row, s_use)

                @block.vector
                def _(q):
                    c = Chain(q, s_c)
                    cnt = MV[:, :, 0]
                    c.step(q.tensor_scalar(cnt, ACC[:, :, D], 1e-8, None, ALU.add))
                    c.step(q.reciprocal(cnt, cnt))
                    c.step(q.tensor_tensor(AD, AD, bcast(cnt.unsqueeze(2), P, NB, D), ALU.mult))
                    for n in range(NCH):
                        q.wait_ge(s_row[n % 2], 16 * (n // 2 + 1))
                        a = ACC[:, n * CH:(n + 1) * CH, 0:D]
                        q.tensor_tensor(a, a, STG[n % 2], ALU.add).then_inc(s_use, 1)
                    q.wait_ge(s_pe, 1)
                    for t, at in ((MEAN, 1), (VAR, 2)):
                        q.wait_ge(s_pe, at)
                        c.step(q.tensor_reduce(t, PS[0][:].rearrange("p (s d) -> p d s", s=4), AX.X, ALU.add))
                        c.step(q.tensor_scalar(t, t, 1.0 / N, None, ALU.mult))
                        if at == 1:
                            q.tensor_tensor(AD, AD, bcast(MEAN.unsqueeze(1), P, NB, D), ALU.subtract).then_inc(s_m, 1)
                    c.step(q.tensor_scalar(VAR, VAR, BN_EPS, None, ALU.add))
                    q.sem_inc(s_p, 1)
                    q.wait_ge(s_sq, NCH + 1)
                    c.step(q.reciprocal(VAR, VAR))
                    q.wait_ge(s_g, 32)
                    c.step(q.tensor_tensor(GAM, GAM, VAR, ALU.mult))
                    c.step(q.tensor_tensor(AD, AD, bcast(GAM.unsqueeze(1), P, NB, D), ALU.mult))
                    c.step(q.tensor_tensor(AD, AD, bcast(BET.unsqueeze(1), P, NB, D), ALU.add))

                @block.tensor
                def _(q):
                    q.wait_ge(s_use, NCH)
                    node_sums(q, AD, list(range(NB)), True, True).then_inc(s_pe, 1)
                    for n in range(NCH):
                        q.wait_ge(s_sq, n + 1)
                        m = node_sums(q, STG[n % 2], list(range(n * CH, (n + 1) * CH)), n == 0, n == NCH - 1)
                        m.then_inc(s_use, 1)
                    q.sem_inc(s_use, 1)
                    m = q.matmul(PS[1][:, 0:1], ONES[:], ONES[:, 0:1], start=True, stop=True)
                    m.then_inc(s_pe, 1)

                @block.scalar
                def _(q):
                    q.wait_ge(s_m, 1)
                    for n in range(NCH):
                        if n >= 2:
                            q.wait_ge(s_use, NCH + n - 1)
                        q.activation(STG[n % 2], ACC[:, n * CH:(n + 1) * CH, 0:D], ACT.Square).then_inc(s_sq, 1)
                    q.wait_ge(s_p, 1)
                    q.activation(VAR, VAR, ACT.Sqrt).then_inc(s_sq, 1)

        PAIRS = K // 2

        def largest_pass(tag):
            fresh()
            s_ids, s_oh, s_v, s_tr, s_red, s_mx, s_c = (own(tag + n) for n in ("ids", "oh", "v", "tr", "red", "mx", "c"))
            s_got, s_st = [sem(tag + f"got{r}") for r in range(RING)], [own(tag + f"st{r}") for r in range(RING)]
            keep = KEEP.rearrange("g p w -> p g w")
            with nc.Block() as block:
                @block.sync
                def _(q):
                    def body(j, r, g):
                        q.wait_ge(s_got[r], 16 * K * (j + 1))
                        q.dma_start(keep[:, bass.ds(g, 1), :], G[:, r, :, :].rearrange("p k w -> p (k w)").unsqueeze(1)).then_inc(s_st[r], 16)
                    groups(q, body)
                    for s in s_st:
                        q.wait_ge(s, 16 * (NG // RING))

                @block.gpsimd
                def _(q):
                    def body(j, r, g):
                        q.wait_ge(s_ids, g + 1)
                        wait(q, s_st[r], 16 * j)
                        wait(q, s_v, (g - RING + 1) * K)
                        q.nop(nofuse=True)
                        gather(q, r, HROW, RW, s_got)
                    groups(q, body)

                @block.scalar
                def _(q):
                    def ids(r, g):
                        q.copy(IDS[:, r, :], IDXB[:, bass.ds(g * K, K)]).then_inc(s_ids, 1)

                    def body(j, r, g):
                        q.wait_ge(s_got[r], 16 * K * (j + 1))
                        q.wait_ge(s_oh, g + 1)
                        for k in range(K):
                            wait(q, s_tr, g * K + k - 3)
                            for hd in range(HEADS):
                                m = q.activation(SCR[:, k % 4, hd * P:(hd + 1) * P], OH[:, r % 2, k, :], ACT.Identity,
                                                 bias=G[:, r, k, D + hd:D + hd + 1], scale=-BIG)
                            m.then_inc(s_v, 1)
                        ids((r + 2) % RING, g + 2)
                    for g in range(2):
                        ids(g, g)
                    groups(q, body)

                @block.tensor
                def _(q):
                    def body(j, r, g):
                        for k in range(K):
                            q.wait_ge(s_v, g * K + k + 1)
                            wait(q, s_red, (g - 1) * PAIRS + k // 2 + 1)
                            for hd in range(HEADS):
                                m = q.transpose(PS[k][:, hd * P:(hd + 1) * P], SCR[:, k % 4, hd * P:(hd + 1) * P], IDENT[:])
                            m.then_inc(s_tr, 1)
                    groups(q, body)

                @block.vector
                def _(q):
                    c = Chain(q, s_c)
                    c.inc(q.memset(MJ[:], -BIG))
                    c.step(q.memset(words, 0.0))

                    def reduced(n):
                        return SM[:, 0, n * 2 * HEADS:(n + 1) * 2 * HEADS]

                    def reduce(g, n):
                        q.wait_ge(s_tr, g * K + 2 * n + 2)
                        wait(q, s_mx, (g - 1) * K + 2 * n + 2)
                        q.tensor_reduce(reduced(n), PSUM[:, n * 1024:(n + 1) * 1024].rearrange("p (h e) -> p h e", e=P), AX.X,
                                        ALU.max).then_inc(s_red, 1)

                    def largest(g, n, regs):
                        wait(q, s_red, g * PAIRS + n + 1)
                        for k in (2 * n, 2 * n + 1):
                            wait(q, s_mx, g * K + k)
                            a = MJW[:, bass.ds(regs[k] * HEADS, HEADS)]
                            q.tensor_tensor(a, a, SM[:, 0, k * HEADS:(k + 1) * HEADS], ALU.max).then_inc(s_mx, 1)

                    def body(j, r, g):
                        regs = blocks(q, BREGB, g)
                        wait(q, s_v, K * g)
                        one_hot(q, r + 1, SLOB, g + 1, ALU.not_equal).then_inc(s_oh, 1)
                        for n in range(PAIRS):
                            reduce(g, n)
                            if n:
                                largest(g, n - 1, regs)
                        largest(g, PAIRS - 1, regs)
                    one_hot(q, 0, SLOB, 0, ALU.not_equal).then_inc(s_oh, 1)
                    groups(q, body)

        def attention_pass(tag):
            fresh()
            s_got = [own(tag + f"got{r}") for r in range(RING)]
            s_c, s_oh, s_tr, s_ot, s_sc, s_z, s_ex, s_wt, s_mm, s_add = (own(tag + n) for n in ("c", "oh", "tr", "ot", "sc", "z", "ex", "wt", "mm", "add"))
            keep = KEEP.rearrange("g p w -> p g w")
            hots = [a.rearrange("p (k n) -> p k n", k=K) for a in
                    (OH[:, 0].rearrange("p k n -> p (k n)"), OH[:, 1].rearrange("p k n -> p (k n)"), POSA[:, 0:K * P], WT[:, 0:K * P])]

            def scores_of(r):
                return PS[6 + r % 2][:, 0:K * 2 * HEADS].rearrange("p (k h) -> p k h", k=K)

            def z_of(r):
                return SM[:, r % 2, :].rearrange("p (k h) -> p k h", k=K)

            with nc.Block() as block:
                @block.sync
                def _(q):
                    def body(j, r, g):
                        wait(q, s_mm, 2 * (g - RING + 1))
                        q.dma_start(G[:, r, :, :].rearrange("p k w -> p (k w)").unsqueeze(1), keep[:, bass.ds(g, 1), :]).then_inc(s_got[r], 16)
                    groups(q, body)

                @block.vector
                def _(q):
                    c = Chain(q, s_c)
                    mi = SI[:, :, HEADS:2 * HEADS]
                    c.step(q.tensor_tensor(mi, SI[:, :, 0:HEADS], MJ[:], ALU.add))
                    c.step(q.scalar_tensor_tensor(mi, mi, SLOPE, mi, ALU.mult, ALU.max))

                    def weights(j, r, g):
                        z = z_of(r)
                        q.wait_ge(s_sc, g + 1)
                        q.wait_ge(s_got[r], 16 * (j + 1))
                        wait(q, s_ex, g - 1)
                        q.tensor_tensor(z, scores_of(r)[:, :, 0:HEADS], G[:, r, :, D:RW], ALU.add).then_inc(s_z, 1)
                        q.wait_ge(s_z, 4 * g + 1)
                        q.scalar_tensor_tensor(z, z, SLOPE, z, ALU.mult, ALU.max).then_inc(s_z, 1)
                        q.wait_ge(s_z, 4 * g + 2)
                        q.tensor_tensor(z, z, scores_of(r)[:, :, HEADS:2 * HEADS], ALU.subtract).then_inc(s_z, 1)
                        q.wait_ge(s_z, 4 * g + 3)
                        q.tensor_scalar(z, z, 0.0, None, ALU.min).then_inc(s_z, 1)

                    def adds(g):
                        regs = blocks(q, BREGB, g)
                        for h in range(2):
                            add_half(q, s_mm, s_add, regs[h * 4:h * 4 + 4], g, h, RW)

                    def next_one_hot(r, g):
                        q.tensor_tensor(hots[r], bcast(IOTA[:].unsqueeze(1), P, K, P),
                                        bcast(SLOB[:, bass.ds(g * K, K)].unsqueeze(2), P, K, P), ALU.is_equal).then_inc(s_oh, 1)

                    def body(j, r, g):
                        next_one_hot((r + 1) % RING, g + 1)
                        weights(j, r, g)
                        if not is_first(g):
                            adds(g - 1)
                    next_one_hot(0, 0)
                    groups(q, body)
                    adds(NG - 1)

                @block.gpsimd
                def _(q):
                    def body(j, r, g):
                        q.wait_ge(s_ex, g + 1)
                        q.nop(nofuse=True)
                        rows = G[:, r, :, 0:D].rearrange("p k (h f) -> p k h f", h=HEADS)
                        q.tensor_tensor(rows, rows, bcast(G[:, r, :, D:RW].unsqueeze(3), P, K, HEADS, HD), ALU.mult).then_inc(s_wt, 1)
                    groups(q, body)

                @block.scalar
                def _(q):
                    def copies(g):
                        for h in range(2):
                            q.wait_ge(s_tr, 2 * g + h + 1)
                            wait(q, s_sc, g)
                            q.copy(SCR[:, h, :], PS[4 + h]).then_inc(s_ot, 1)

                    def body(j, r, g):
                        q.wait_ge(s_z, 4 * g + 4)
                        q.activation(G[:, r, :, D:RW], z_of(r), ACT.Exp).then_inc(s_ex, 1)
                        copies(g + 1)
                    copies(0)
                    groups(q, body)

                @block.tensor
                def _(q):
                    q.wait_ge(s_c, 2)

                    def scores(r, g):
                        regs = blocks(q, BREGB, g)
                        q.wait_ge(s_oh, g + 1)
                        for h in range(2):
                            wait(q, s_ot, 2 * g + h - 1)
                            for k in range(4):
                                m = q.transpose(PS[4 + h][:, k * P:(k + 1) * P], hots[r][:, h * 4 + k, :], IDENT[:])
                            m.then_inc(s_tr, 1)
                        wait(q, s_z, 4 * (g - 1) - 1)
                        for h in range(2):
                            q.wait_ge(s_ot, 2 * g + h + 1)
                            for k in range(4):
                                m = q.matmul(scores_of(r)[:, h * 4 + k, :], SCR[:, h, k * P:(k + 1) * P],
                                             SIW[:, bass.ds(regs[h * 4 + k] * 2 * HEADS, 2 * HEADS)], start=True, stop=True)
                        m.then_inc(s_sc, 1)

                    def body(j, r, g):
                        scores((r + 1) % RING, g + 1)
                        q.wait_ge(s_wt, g + 1)
                        for h in range(2):
                            wait(q, s_add, (g - 1) * K + (h + 1) * K // 2)
                            for k in range(h * 4, h * 4 + 4):
                                m = q.matmul(slot(k), hots[r][:, k, :], G[:, r, k, :], start=True, stop=True)
                            m.then_inc(s_mm, 1)
                    scores(0, 0)
                    groups(q, body)

        dense("d0", True, load_relations(W1, loop1, b1), (R + 1) * D, R * D, True)
        sum_pass("g0", TAB, D, D, True)
        dense("d1", False, load_relations(W2, loop2, b2), (R + 1) * D, R * D, True)
        sum_pass("g1", TAB, D, D, False)

        def load_square(W, bias, more=None):
            def load(q, s):
                q.dma_start(WT[:, 0:D], W).then_inc(s, 16)
                q.dma_start(BIAS[:, 0:D], bias.partition_broadcast(P)).then_inc(s, 16)
                if more is not None:
                    q.dma_start(GW[:, 0:2 * D], more.rearrange("a h f -> (a h f)").partition_broadcast(P)).then_inc(s, 16)
            load.total = 48 if more is not None else 32
            return load

        def add_to_x(q, c):
            c.step(q.tensor_tensor(X[:], X[:], AD, ALU.add))
            c.step(q.memset(ACC[:, :, D:RW], 0.0))

        dense("d2", True, load_square(lw, lb), D, 0, False, before=add_to_x)
        scatter_pass("sc")
        message_pass("ms", D + 1)
        batch_norm_stage("bn")
        def project_attention(q, c, s_w):
            q.wait_ge(s_w, 48)
            a = GW[:, 0:2 * D].rearrange("p (h f) -> p h f", h=HEADS)
            t = GW[:, 2 * D:3 * D].rearrange("p (h f) -> p h f", h=HEADS)
            for m in (WT, BIAS):
                for at, f0 in ((D, HD), (RW, 0)):
                    c.step(q.tensor_tensor(t, m[:, 0:D].rearrange("p (h f) -> p h f", h=HEADS), a[:, :, f0:f0 + HD], ALU.mult))
                    c.step(q.tensor_reduce(m[:, at:at + HEADS], t, AX.X, ALU.add))

        dense("d3", True, load_square(gw, gb, attn), RW + HEADS, 0, False, before=lambda q, c: c.step(q.tensor_tensor(X[:], X[:], AD, ALU.add)),
              prepare=project_attention)
        largest_pass("lp")
        attention_pass("at")
        fresh()
        s_row, s_use, s_c, s_var, s_std, s_norm, s_h, s_o = ([own("f_row0"), own("f_row1")], own("f_use"), own("f_c"), own("f_var"), own("f_std"),
                                                             own("f_norm"), own("f_h"), own("f_o"))
        with nc.Block() as block:
            @block.sync
            def _(q):
                load_rows(q, s_row, s_use)
                q.wait_ge(s_h, 1 + NB)
                q.dma_start(HROWV, ACC[:]).then_inc(s_o, 16)
                q.wait_ge(s_o, 16)

            @block.vector
            def _(q):
                c = Chain(q, s_c)
                den = MJ[:]
                c.step(q.tensor_scalar(den, ACC[:, :, D:RW], 1e-30, None, ALU.max))
                c.step(q.reciprocal(den, den))
                sums4 = AD.rearrange("p b (h f) -> p b h f", h=HEADS)
                c.step(q.tensor_tensor(sums4, sums4, bcast(den.unsqueeze(3), P, NB, HEADS, HD), ALU.mult))
                c.step(q.tensor_tensor(X[:], X[:], AD, ALU.add))
                for n in range(NCH):
                    q.wait_ge(s_row[n % 2], 16 * (n // 2 + 1))
                    a = X[:, n * CH:(n + 1) * CH, :]
                    q.tensor_tensor(a, a, STG[n % 2], ALU.add).then_inc(s_use, 1)
                q.wait_ge(s_use, NCH)
                norm_vector(q, c, s_var, s_std, s_norm)
                c.inc(q.memset(ACC[:, :, D + 1:RW], 0.0))
                c.inc(q.memset(ACC[:, :, D:D + 1], 1.0))
                c.inc(q.tensor_scalar(IDXA[:], IDXA[:], 3, None, ALU.arith_shift_right))
                c.hold()
                q.sem_inc(s_h, 1)

            @block.scalar
            def _(q):
                norm_scalar(q, s_var, s_std, s_norm)
                with q.Fori(0, NB) as b:
                    q.activation(words[:, bass.ds(b * RW, D)], XW[:, bass.ds(b * D, D)], ACT.Relu,
                                 bias=NMR[:, bass.ds(b, 1)], scale=RSTD[:, bass.ds(b, 1)]).then_inc(s_h, 1)
        with nc.Block() as block:
            s_z = own("f_z")

            @block.vector
            def _(q):
                q.memset(words, 0.0).then_inc(s_z, 1)
        sum_pass("g3", HROW, RW, D + 1, False)
        fresh()
        s_c, s_f, s_o = own("e_c"), own("e_f"), own("e_o")
        with nc.Block() as block:
            @block.vector
            def _(q):
                c = Chain(q, s_c)
                cnt = MV[:, :, 0]
                c.step(q.tensor_scalar(cnt, ACC[:, :, D], 1.0, None, ALU.max))
                c.step(q.reciprocal(cnt, cnt))
                c.step(q.tensor_tensor(AD, AD, bcast(cnt.unsqueeze(2), P, NB, D), ALU.mult))
                q.tensor_tensor(X[:], X[:], AD, ALU.add).then_inc(s_f, 1)

            @block.sync
            def _(q):
                q.wait_ge(s_f, 1)
                q.dma_start(out[0:(NB - 1) * P, :].rearrange("(b p) d -> p b d", p=P), X[:, 0:NB - 1, :]).then_inc(s_o, 16)
                q.dma_start(out[(NB - 1) * P:N, :], X[0:LAST, NB - 1, :]).then_inc(s_o, 16)
                q.wait_ge(s_o, 32)


_INS = ['x', 'src', 'dst', 'edge_type_8', 'L0_gnn_W1', 'L0_gnn_loop1', 'L0_gnn_b1', 'L0_gnn_W2', 'L0_gnn_loop2',
        'L0_gnn_b2', 'L1_gnn_W', 'L1_gnn_b', 'L1_gnn_gamma', 'L1_gnn_beta', 'L2_gnn_W', 'L2_gnn_b', 'L2_gnn_attn']


def kernel(**inputs):
    import numpy as np
    import concourse.bacc as bacc
    from concourse.bass_utils import run_bass_kernel_spmd

    nc = bacc.Bacc("TRN2", target_bir_lowering=False, num_devices=1)
    arrays, args = {}, []
    for name in _INS:
        a = np.asarray(inputs[name])
        if name == 'L1_gnn_W':
            a = a.T
        arrays[f"in_{name}"] = a = np.ascontiguousarray(a)
        args.append(nc.dram_tensor(f"in_{name}", a.shape, mybir.dt.from_np(a.dtype), kind="ExternalInput").ap())
    out = nc.dram_tensor("out", (N, D), F32, kind="ExternalOutput").ap()
    build_gnn(nc, *args, out)
    return run_bass_kernel_spmd(nc, [arrays], core_ids=[0]).results[0]["out"]
```
